# Optimizing a Trainium2 kernel written in Bass

```python
import numpy as np
import jax
import jax.numpy as jnp

def _softmax(x, axis=-1):
    return jax.nn.softmax(x, axis=axis)

def _gelu(x):
    return jax.nn.gelu(x, approximate=True)

def _silu(x):
    return jax.nn.silu(x)

def _sigmoid(x):
    return jax.nn.sigmoid(x)

def _layernorm(x, axis=-1, eps=1e-05):
    m = jnp.mean(x, axis=axis, keepdims=True)
    v = jnp.var(x, axis=axis, keepdims=True)
    return (x - m) / jnp.sqrt(v + eps)

def _scatter_add(tgt, idx, src, axis=0):
    return tgt.at[idx].add(src)

def _segment_sum(src, seg, n):
    return jax.ops.segment_sum(src, seg, n)
kernel_name = 'mk_flamingo_gated_d1_seqx_r4_e9f7d0'

def setup_inputs(seed: int=0):
    np.random.seed(seed)
    _w = jnp.asarray

    def _rec_inputs():
        import jax
        import jax.numpy as jnp
        _rk = jax.random.key(seed)
        x = -0.0002928 + 1 * jax.random.normal(jax.random.fold_in(_rk, 1), (4, 512, 256), jnp.float32)
        _lenS = 512 - jax.random.randint(jax.random.fold_in(_rk, 7), (4,), 0, max(1, 512 // 4) + 1, jnp.int32)
        _lenS2 = 512 - jax.random.randint(jax.random.fold_in(_rk, 8), (4,), 0, max(1, 512 // 4) + 1, jnp.int32)
        _ctx_1024P = jax.random.normal(jax.random.fold_in(_rk, 11), (4, 16, 256), jnp.float32)
        _ctx_1024c = jax.random.dirichlet(jax.random.fold_in(_rk, 511), 0.3 * jnp.ones((16,), jnp.float32), (4, 512))
        _ctx_1024t = jnp.einsum('bsk,bkd->bsd', _ctx_1024c, _ctx_1024P)
        _ctx_1024t = _ctx_1024t * jax.lax.rsqrt(jnp.mean(jnp.square(_ctx_1024t)) + 1e-12) * 0.953939
        ctx_1024 = -1.39393e-06 + 0.999914 * (_ctx_1024t + 0.3 * jax.random.normal(jax.random.fold_in(_rk, 611), (4, 512, 256), jnp.float32))
        _validS = jnp.arange(512)[None, :] < _lenS[:, None]
        _validS2 = jnp.arange(512)[None, :] < _lenS2[:, None]
        _causal = jnp.tril(jnp.ones((512, 512), dtype=bool))
        mask_Bx1xSxS2_ik1 = jnp.where(jnp.broadcast_to(_validS2[:, None, None, :], (4, 1, 512, 512)), 1, 0).astype(jnp.int32)
        _g = jax.random.normal(jax.random.fold_in(_rk, 9001), (2, 1), jnp.float32)
        _g = jnp.sign(_g) * jnp.maximum(jnp.abs(_g), 1.0) + (_g == 0) * 1.0
        g_xattn = _g[0]
        g_ffn = _g[1]
        return (x, ctx_1024, mask_Bx1xSxS2_ik1, g_xattn, g_ffn)
    x, ctx_1024, mask_Bx1xSxS2_ik1, g_xattn, g_ffn = _rec_inputs()

    def _L0_xattn_setup():
        import jax, jax.numpy as jnp
        import numpy as np
        B, S, E, H = (2, 512, 256, 16)
        D = E // H
        key = jax.random.key(seed)
        ks = jax.random.split(key, 14)
        inp = {'query': jax.random.normal(ks[0], (B, S, E), jnp.float32), 'key': jax.random.normal(ks[1], (B, S, E), jnp.float32), 'value': jax.random.normal(ks[2], (B, S, E), jnp.float32), 'adj': jax.random.normal(ks[3], (S, S), jnp.float32), 'mask': jax.random.randint(ks[4], (B, 1, S, S), 0, 2, jnp.int32)}
        sc = 1.0 / np.sqrt(E)
        inp['Wq'] = jax.random.normal(ks[5], (E, E), jnp.float32) * sc
        inp['bq'] = jax.random.normal(ks[6], (E,), jnp.float32) * sc
        inp['Wk'] = jax.random.normal(ks[7], (E, E), jnp.float32) * sc
        inp['bk'] = jax.random.normal(ks[8], (E,), jnp.float32) * sc
        inp['Wv'] = jax.random.normal(ks[9], (E, E), jnp.float32) * sc
        inp['bv'] = jax.random.normal(ks[10], (E,), jnp.float32) * sc
        inp['Wo'] = jax.random.normal(ks[11], (E, E), jnp.float32) * sc
        inp['bo'] = jax.random.normal(ks[12], (E,), jnp.float32) * sc
        return inp
    _L0_xattn_all = _L0_xattn_setup()
    _L0_xattn_in = {k: v for k, v in _L0_xattn_all.items() if k in ('adj', 'Wq', 'bq', 'Wk', 'bk', 'Wv', 'bv', 'Wo', 'bo')}
    del _L0_xattn_all

    def _L0_ffn_setup():
        import jax, jax.numpy as jnp
        import numpy as np
        B, S, H, E, DFF = (4, 1024, 256, 8, 1024)
        key = jax.random.key(seed)
        k0, k1, k2, k3 = jax.random.split(key, 4)
        hidden_states = jax.random.normal(k0, (B, S, H), dtype=jnp.float32)
        gate_w = jax.random.normal(k1, (E, H), dtype=jnp.float32) * 0.02
        w1 = jax.random.normal(k2, (E, H, DFF), dtype=jnp.float32) * 0.02
        b1 = jnp.zeros((E, DFF), dtype=jnp.float32)
        w2 = jax.random.normal(k3, (E, DFF, H), dtype=jnp.float32) * 0.02
        b2 = jnp.zeros((E, H), dtype=jnp.float32)
        return {'hidden_states': hidden_states, 'gate_w': gate_w, 'w1': w1, 'b1': b1, 'w2': w2, 'b2': b2}
    _L0_ffn_all = _L0_ffn_setup()
    _L0_ffn_in = {k: v for k, v in _L0_ffn_all.items() if k in ('gate_w', 'w1', 'b1', 'w2', 'b2')}
    del _L0_ffn_all
    return {'x': x, 'ctx_1024': ctx_1024, 'mask_Bx1xSxS2_ik1': mask_Bx1xSxS2_ik1, 'g_xattn': g_xattn, 'g_ffn': g_ffn, 'L0_xattn_adj': _L0_xattn_in['adj'], 'L0_xattn_Wq': _L0_xattn_in['Wq'], 'L0_xattn_bq': _L0_xattn_in['bq'], 'L0_xattn_Wk': _L0_xattn_in['Wk'], 'L0_xattn_bk': _L0_xattn_in['bk'], 'L0_xattn_Wv': _L0_xattn_in['Wv'], 'L0_xattn_bv': _L0_xattn_in['bv'], 'L0_xattn_Wo': _L0_xattn_in['Wo'], 'L0_xattn_bo': _L0_xattn_in['bo'], 'L0_ffn_gate_w': _L0_ffn_in['gate_w'], 'L0_ffn_w1': _L0_ffn_in['w1'], 'L0_ffn_b1': _L0_ffn_in['b1'], 'L0_ffn_w2': _L0_ffn_in['w2'], 'L0_ffn_b2': _L0_ffn_in['b2']}

def reference(x, ctx_1024, mask_Bx1xSxS2_ik1, g_xattn, g_ffn, L0_xattn_adj, L0_xattn_Wq, L0_xattn_bq, L0_xattn_Wk, L0_xattn_bk, L0_xattn_Wv, L0_xattn_bv, L0_xattn_Wo, L0_xattn_bo, L0_ffn_gate_w, L0_ffn_w1, L0_ffn_b1, L0_ffn_w2, L0_ffn_b2):
    import jax
    import jax.numpy as jnp

    def _L0_xattn_ref(query, key, value, adj, mask, Wq, bq, Wk, bk, Wv, bv, Wo, bo):
        import jax, jax.numpy as jnp
        import numpy as np
        B, S, E, H = (2, 512, 256, 16)
        D = E // H
        b, s, _ = query.shape

        def heads(x, W, bias):
            y = jnp.einsum('bse,ef->bsf', x, W.T) + bias
            return y.reshape(b, s, H, D).transpose(0, 2, 1, 3)
        Q = heads(query, Wq, bq)
        K = heads(key, Wk, bk)
        V = heads(value, Wv, bv)
        scores = jnp.einsum('bhqd,bhkd->bhqk', Q, K) / jnp.sqrt(jnp.float32(D))
        scores = scores + adj[None, None, :, :]
        scores = jnp.where(mask == 0, jnp.float32(-jnp.inf), scores)
        weights = jax.nn.softmax(scores, axis=-1)
        out = jnp.einsum('bhqk,bhkd->bhqd', weights, V)
        out = out.transpose(0, 2, 1, 3).reshape(b, s, E)
        return jnp.einsum('bse,ef->bsf', out, Wo.T) + bo

    def _L0_ffn_ref(hidden_states, gate_w, w1, b1, w2, b2):
        import jax, jax.numpy as jnp
        import numpy as np
        B, S, H, E, DFF = (4, 1024, 256, 8, 1024)
        b, s, h = hidden_states.shape
        x = hidden_states.reshape(-1, h)
        gate_logits = x @ gate_w.T
        gate_probs = jax.nn.softmax(gate_logits, axis=-1)
        expert_idx = jnp.argmax(gate_probs, axis=-1)
        expert_w = jnp.take_along_axis(gate_probs, expert_idx[:, None], axis=1)[:, 0]
        out = jnp.zeros_like(x)
        n_experts = w1.shape[0]
        for e in range(n_experts):
            ye = jax.nn.relu(x @ w1[e] + b1[e]) @ w2[e] + b2[e]
            sel = (expert_idx == e)[:, None]
            out = out + jnp.where(sel, ye * expert_w[:, None], 0.0)
        return out.reshape(b, s, h)
    x = x + jnp.tanh(g_xattn[0]) * _L0_xattn_ref(_layernorm(x, axis=-1), ctx_1024, ctx_1024, L0_xattn_adj, mask_Bx1xSxS2_ik1, L0_xattn_Wq, L0_xattn_bq, L0_xattn_Wk, L0_xattn_bk, L0_xattn_Wv, L0_xattn_bv, L0_xattn_Wo, L0_xattn_bo)
    x = x + jnp.tanh(g_ffn[0]) * _L0_ffn_ref(_layernorm(x, axis=-1), L0_ffn_gate_w, L0_ffn_w1, L0_ffn_b1, L0_ffn_w2, L0_ffn_b2)
    return x

_drawn_inputs = setup_inputs


def setup_inputs(seed=0):
    import zlib

    import numpy as np

    out = dict(_drawn_inputs(seed))
    spreads = {'L0_ffn_b1': (0.0, 0.8), 'L0_ffn_b2': (0.0, 0.445)}
    factors = {'L0_xattn_bq': 5.13, 'L0_xattn_bk': 8.0}
    for name, (base, spread) in spreads.items():
        noise = np.random.default_rng([zlib.crc32(name.encode()), seed]).standard_normal(out[name].shape)
        drawn = base * np.exp(spread * noise) if base else spread * noise
        out[name] = jnp.asarray(drawn.astype(out[name].dtype))
    for name, factor in factors.items():
        out[name] = (out[name] * factor).astype(out[name].dtype)
    return out
```

```python
from contextlib import ExitStack

import concourse.bass as bass
from concourse import mybir

ALU = mybir.AluOpType
ACT = mybir.ActivationFunctionType
AX = mybir.AxisListType
F32 = mybir.dt.float32
BF16 = mybir.dt.bfloat16
I32 = mybir.dt.int32
ds = bass.ds

P = 128
EPS = 1e-5
SHUT = -1e30
BIG = 3e38

Q_PART = [0, 0, 1, 1, 0, 2, 1, 2]
K_PART = [0, 1, 0, 1, 2, 0, 2, 1]
PAIRS = len(Q_PART)


def build(nc, x, ctx_in, mask, g_xattn, g_ffn, adj, Wq, bq, Wk, bk, Wv, bv, Wo, bo,
          gate_w, w1, b1, w2, b2, out):
    B, S, E = x.shape
    X, _, DFF = w1.shape
    D = P // PAIRS
    H = E // D
    QT = S // P
    EC = E // P
    FC = DFF // P
    TOK = B * S
    NT = TOK // P
    SLOTS = NT + X - 1
    SLOTS_R = SLOTS + SLOTS % 2
    HG = 4
    NG = H // HG
    QH = 2
    GROUPS = QH * NG
    QPG = QT // QH
    TPG = QPG * HG
    TILES = GROUPS * TPG
    HALF = S // QH
    VW = 32
    assert (D, H, E, S) == (16, 16, 256, 512)

    NB = 6
    NS = 3
    NTB = 2
    LT = 4
    LE = 4
    LP = LE + 1
    DVE_COPIES = (1, 4, 6)

    def dve_copies(n):
        return sum(1 for i in range(n) if i % 8 in DVE_COPIES)

    def act_copies(n):
        return n - dve_copies(n)

    SETUP_USES = 6
    BATCH_USES = 10

    def pro_use(b, i):
        return SETUP_USES + BATCH_USES * b + i

    def val_use(b, i):
        return SETUP_USES + 8 + BATCH_USES * b + i

    def half(v, k):
        return v * (BATCH_USES // 2) + k // 2

    with ExitStack() as st:
        def sb(name, shape, dt=F32):
            return st.enter_context(nc.sbuf_tensor(name, shape, dt))

        def sem(name):
            return st.enter_context(nc.semaphore(name))

        w2s = sb("w2s", [P, X, FC, E])
        stack = w2s[:].rearrange("p x c e -> p (x c e)").bitcast(BF16).rearrange(
            "p (b t h s) -> p b t h s", b=2, t=2, h=H)
        pt = sb("pt", [P, 2, QT, HG, HALF])
        pt_flat = pt[:].rearrange("p a c j q -> p (a c j q)")
        wraw = pt_flat[:, 0:4 * EC * E].rearrange("p (w m e) -> p w m e", w=4, m=EC)
        w1s = pt_flat.rearrange("p (u k f) -> p u k f", u=4, k=EC)
        prob = sb("prob", [P, NB, S])
        negmax = sb("negmax", [P, NB])
        vals = sb("vals", [P, QT, H, VW])
        o_sb = sb("o_sb", [P, NG, TOK])
        adjm = sb("adjm", [P, QT, S])
        maski = sb("maski", [P, QT, S], I32)
        xin = sb("xin", [P, QT, E])
        cin = sb("cin", [P, QT, E])
        xT = sb("xT", [P, EC, S])
        cT = sb("cT", [P, EC, S])
        parts = sb("parts", [P, 2, EC, 3, S], BF16)
        rest = sb("rest", [P, S])
        wT = sb("wT", [P, 4, EC, E])
        minus_half = sb("minus_half", [P, QT])
        ident = sb("ident", [P, P])
        stats = sb("stats", [P, QT, 6])
        mv = sb("mv", [P, QT, 2])
        rstd = sb("rstd", [P, QT])
        early = o_sb[:].rearrange("p a t -> p (a t)")
        zrow = early[0:1, 0:2 * E]
        gate_r = early[0:X, 2 * E:3 * E]
        rowsm = early[0:X * FC + 2 * EC, 3 * E:3 * E + P]
        colsm = sb("colsm", [P, X * FC + 4])
        gateT = sb("gateT", [P, EC, X])
        bvb = sb("bvb", [P, E])
        bob = sb("bob", [P, E])
        gr = sb("gr", [P, 2])
        tg = sb("tg", [P, 2])
        logit = sb("logit", [P, NT, X])
        b1c = colsm[:, 0:X * FC]
        bqc = colsm[:, X * FC:X * FC + EC]
        bkc = colsm[:, X * FC + EC:X * FC + 2 * EC]
        oc = parts[:].rearrange("p t m a s -> p (t m a s)").bitcast(F32)[:, 0:2 * NG * P].rearrange(
            "p (u a q) -> p u a q", u=2, a=NG)
        xres = xin[:, 0:2, :]
        attn = cin[:, 0:2, :]
        atT = xT[:].rearrange("p k (u q) -> p u k q", u=4)[:, 0:2]
        x2T = cT[:].rearrange("p k (u q) -> p u k q", u=4)[:, 0:2]
        rows = adjm[:].rearrange("p t s -> p (t s)").rearrange("p (u s) -> p u s", u=4)
        b2b = maski[:].rearrange("p t s -> p (t s)").bitcast(F32).rearrange("p (x e) -> p x e", x=X)
        rt_flat = prob[:].rearrange("p n s -> p (n s)")
        hT = o_sb[:].rearrange("p a t -> p (a t)")[:, 0:2 * FC * P].rearrange(
            "p (u c t) -> p u c t", u=2, c=FC)
        xgT = o_sb[:].rearrange("p a t -> p (a t)")[:, 2 * FC * P:2 * FC * P + 4 * P].rearrange(
            "p (u k t) -> p u k t", u=2, k=EC)
        orow = o_sb[:].rearrange("p a t -> p (a t)")[:, 3072:3072 + 2 * E].rearrange(
            "p (u e) -> p u e", u=2)
        ytmp = o_sb[:].rearrange("p a t -> p (a t)")[:, 4096:4096 + 2 * E].rearrange(
            "p (u e) -> p u e", u=2)
        rinv = sb("rinv", [P, 2, H])
        st2 = sb("st2", [P, 2, 6])
        mv2 = sb("mv2", [P, 2, 2])
        rstd2 = sb("rstd2", [P, 2])
        pair = sb("pair", [P, NT, 2], I32)
        posi = sb("posi", [P, NT], I32)
        slots = sb("slots", [P, SLOTS_R, 2], I32)
        eid = sb("eid", [P, SLOTS_R], I32)
        gidx = sb("gidx", [P, 2], I32)
        sidx = sb("sidx", [P, 2], I32)
        ltri = sb("ltri", [P, P])
        ones = sb("ones", [P, P])
        seven = sb("seven", [P, X])
        thr = sb("thr", [P, NT])
        slotn = sb("slotn", [P, SLOTS_R])

        bank = [st.enter_context(nc.psum_tensor(f"bank{i}", [P, 512], F32)) for i in range(8)]
        sc_bank, tr_bank, pv_bank, sp_bank = bank[0:NS], bank[NS:NS + NTB], bank[5], bank[6:8]

        part_d = nc.dram_tensor("part_d", [2, 2, 3, E, S], BF16, kind="Internal").ap()
        rows_d = nc.dram_tensor("rows_d", [TOK + 1, 2 * E], F32, kind="Internal").ap()
        slot_d = nc.dram_tensor("slot_d", [SLOTS_R * P, 2], I32, kind="Internal").ap()

        x_v = x.rearrange("b (t p) e -> b p t e", p=P)
        c_v = ctx_in.rearrange("b (t p) e -> b p t e", p=P)
        m_v = mask.rearrange("b o (t p) s -> b p (o t) s", p=P)
        adj_v = adj.rearrange("(t p) s -> p t s", p=P)
        xt_v = x.rearrange("b (t p) e -> (b t) p e", p=P)
        out_v = out.rearrange("b s e -> (b s) e")
        w1_v = w1.rearrange("x (k p) f -> x p k f", p=P)

        (s_wraw, s_small, s_bcast, s_x, s_ctx, s_mask, s_const, s_m, s_stat, s_mv, s_rstd,
         s_xn, s_p0, s_rest, s_p1, s_parts, s_stack, s_adjm, s_penal, s_v, s_score,
         s_masked, s_exp, s_trans, s_cact, s_cdve, s_pv, s_osb, s_tg, s_vinit) = [
            sem(n) for n in (
                "wraw", "small", "bcast", "x", "ctx", "mask", "const", "m", "stat", "mv",
                "rstd", "xn", "p0", "rest", "p1", "parts", "stack", "adjm", "penal", "v",
                "score", "masked", "exp", "trans", "cact", "cdve", "pv", "osb", "tg", "vinit")]
        s_waited = [sem("waited0"), sem("waited1")]
        s_partd, s_adj, t_x = ([sem(f"{n}{k}") for k in range(2)] for n in ("partd", "adj", "t_xres"))
        r_fill, f_free = sem("r_fill"), sem("f_free")
        s_eps, t_eps, s_half = sem("eps"), sem("t_eps"), sem("half")
        s_md = [sem("md0"), sem("md1")]
        (t_oc, t_ot, t_rinv, t_attn, t_at, t_atT, t_op, t_y, t_x1, t_stat, t_mv, t_rstd,
         t_row, t_out, t_x2, t_x2T, t_lg, t_logit) = [
            sem("t_" + n) for n in (
                "oc", "ot", "rinv", "attn", "at", "atT", "op", "y", "x1", "stat", "mv",
                "rstd", "row", "out", "x2", "x2T", "lg", "logit")]
        (r_dve, r_exp, r_sub, r_oh, r_rank, r_pos, r_pair, r_scat, r_slots, r_init, r_eid, r_w2,
         r_b2) = [sem("r_" + n) for n in (
             "dve", "exp", "sub", "oh", "rank", "pos", "pair", "scat", "slots", "init", "eid",
             "w2", "b2")]
        (f_xt, f_xgT, f_h, f_hT, f_y, f_tmp, f_out, f_gi, f_si) = [
            sem("f_" + n) for n in ("xt", "xgT", "h", "hT", "y", "tmp", "out", "gi", "si")]
        f_w1 = [sem("f_w1_0"), sem("f_w1_1")]
        f_row = [sem("f_row0"), sem("f_row1")]
        f_sc = [sem("f_sc0"), sem("f_sc1")]

        block = st.enter_context(nc.Block())

        def wait_apart(eng, s, value):
            eng.wait_ge(s, value)
            eng.sem_inc(s_waited[eng is nc.vector], 1)

        def tile_of(n):
            g, r = divmod(n, TPG)
            qh, hg = divmod(g, NG)
            q2, j = divmod(r, HG)
            return g, qh * QPG + q2, q2, hg * HG + j, j

        @block.sync
        def _(sp):
            for n, w in enumerate((Wq, Wk, Wv, Wo)):
                sp.dma_start(wraw[:, n], w.rearrange("(m p) e -> p m e", p=P)).then_inc(s_wraw, 16)
            sp.dma_start(xin[:], x_v[0]).then_inc(s_x, 16)
            sp.dma_start(cin[:], c_v[0]).then_inc(s_ctx, 16)
            sp.dma_start(rowsm[0:X * FC, :], b1.rearrange("x (c p) -> (x c) p", p=P)).then_inc(s_small, 16)
            sp.dma_start(rowsm[X * FC:X * FC + EC, :], bq.rearrange("(c p) -> c p", p=P)).then_inc(s_small, 16)
            sp.dma_start(rowsm[X * FC + EC:X * FC + 2 * EC, :], bk.rearrange("(c p) -> c p", p=P)).then_inc(s_small, 16)
            sp.dma_start(gate_r, gate_w).then_inc(s_small, 16)
            sp.dma_start(maski[:], m_v[0]).then_inc(s_mask, 16)

            def load_adj(q0, q1):
                sp.dma_start(adjm[:, q0:q1], adj_v[:, q0:q1]).then_inc(s_adj[q0 > 0], 16)

            load_adj(0, QT // 2)
            load_adj(QT // 2, QT)
            for dst, src in ((bvb[:], bv), (bob[:], bo)):
                sp.dma_start(dst, src.rearrange("(o e) -> o e", o=1).to_broadcast([P, E])).then_inc(s_bcast, 16)
            for n, g in enumerate((g_xattn, g_ffn)):
                sp.dma_start(gr[:, n:n + 1], g.rearrange("(o e) -> o e", o=1).to_broadcast([P, 1])).then_inc(s_bcast, 16)

            def stack_parts(b, par):
                for t in range(2):
                    for m in range(EC):
                        sp.wait_ge(s_parts, b * 4 + (2 * t + m + 1))
                        sp.dma_start(part_d[par, t, :, m * P:(m + 1) * P, :].rearrange("o a p s -> p (o a) s"),
                                     parts[:, t, m]).then_inc(s_partd[t], 16)
                for t in range(2):
                    sp.wait_ge(s_partd[t], b * 32 + 32)
                    for j, part in enumerate((Q_PART, K_PART)[t]):
                        sp.dma_start(stack[D * j:D * (j + 1), par, t].rearrange("p o h s -> p (o h) s"),
                                     part_d[par, t, part].rearrange("o (h d) s -> d (o h) s", d=D)
                                     ).then_inc(s_stack, 16)

            stack_parts(0, ds(0, 1))
            with sp.Fori(0, B - 1) as b:
                sp.wait_ge(s_m, pro_use(b, 2))
                sp.dma_start(xin[:], x_v[ds(b + 1, 1)].rearrange("b p t e -> p (b t) e")).then_inc(s_x, 16)
                sp.wait_ge(s_m, pro_use(b, 4))
                sp.dma_start(cin[:], c_v[ds(b + 1, 1)].rearrange("b p t e -> p (b t) e")).then_inc(s_ctx, 16)
                sp.wait_ge(s_adjm, b * QT + QT)
                sp.dma_start(maski[:], m_v[ds(b + 1, 1)].rearrange("b p t e -> p (b t) e")).then_inc(s_mask, 16)
                stack_parts(b + 1, ds((b + 1) % 2, 1))
                sp.wait_ge(s_masked, b * TILES + TILES // 2)
                load_adj(0, QT // 2)
                sp.wait_ge(s_masked, b * TILES + TILES)
                load_adj(QT // 2, QT)

            sp.wait_ge(s_osb, B * GROUPS)
            for e in range(X):
                sp.dma_start(w2s[:, e], w2[e].rearrange("(c p) f -> p c f", p=P)).then_inc(r_w2, 16)
            sp.wait_ge(s_adjm, B * QT)
            sp.dma_start(b2b, b2.rearrange("(o x) e -> o (x e)", o=1).to_broadcast([P, X * E]).rearrange(
                "p (x e) -> p x e", x=X)).then_inc(r_b2, 16)
            with sp.Fori(0, NT // 2) as i:
                for u in range(2):
                    sp.wait_ge(t_x1, i * 2 + u + 1)
                    sp.dma_start(xres[:, u], xt_v[ds(i * 2 + u, 1)].rearrange("b p e -> p (b e)")).then_inc(t_x[u], 16)
                for u in range(2):
                    sp.wait_ge(t_row, i * 2 + u + 1)
                    sp.dma_start(rows_d[ds(i * 2 * P + u * P, P), :], rows[:, u]).then_inc(t_out, 16)
            sp.wait_ge(r_scat, 16 * NT)
            sp.dma_start(slots[:], slot_d.rearrange("(s p) a -> p s a", p=P)).then_inc(r_slots, 16)
            sp.wait_ge(r_eid, 1)

            def load_w1(s, u):
                e = sp.value_load(eid[0:1, ds(s, 1)], min_val=0, max_val=X - 1)
                sp.dma_start(w1s[:, u], w1_v[ds(e, 1)].rearrange("x p k f -> p (x k) f")).then_inc(f_w1[u], 16)

            for u in range(2):
                load_w1(u, u)
            with sp.Fori(0, (SLOTS - 3) // 2) as i:
                for u in range(2):
                    sp.wait_ge(f_h, i * (2 * FC) + FC * (u + 1))
                    load_w1(i * 2 + (u + 2), u)
            sp.wait_ge(f_h, FC * (SLOTS - 2))
            load_w1(SLOTS - 1, 0)
            for u in range(2):
                sp.wait_ge(f_sc[u], 16 * ((SLOTS + 1 - u) // 2))

        @block.gpsimd
        def _(po):
            po.memset(ident[:], 0.0).then_inc(s_const, 1)
            po.memset(ones[:], 1.0).then_inc(s_const, 1)
            po.memset(minus_half[:], -0.5).then_inc(s_half, 1)
            po.memset(vals[:], 0.0).then_inc(s_vinit, 1)
            po.wait_ge(s_const, 2)
            po.affine_select(out=ident[:], in_=ident[:], compare_op=ALU.not_equal, fill=1.0, base=0,
                             pattern=[[-1, P]], channel_multiplier=1).then_inc(s_const, 1)
            po.wait_ge(s_vinit, 1)
            po.memset(vals[:, :, :, D:D + 1], 1.0).then_inc(s_vinit, 1)
            po.affine_select(out=ltri[:], in_=ones[:], compare_op=ALU.is_gt, fill=0.0, base=0,
                             pattern=[[1, P]], channel_multiplier=-1).then_inc(s_const, 1)
            po.iota(pair[:, :, 0], pattern=[[P, NT]], base=0, channel_multiplier=1).then_inc(s_const, 1)
            po.iota(posi[:, 0:X], pattern=[[-1, X]], base=X, channel_multiplier=0).then_inc(s_const, 1)
            po.wait_ge(s_const, 6)
            po.tensor_copy(seven[:], posi[:, 0:X]).then_inc(s_const, 1)
            po.wait_ge(s_const, 7)
            po.iota(posi[:], pattern=[[P, NT]], base=0, channel_multiplier=0).then_inc(s_const, 1)
            po.wait_ge(s_const, 8)
            po.tensor_copy(thr[:], posi[:]).then_inc(s_const, 1)
            po.iota(eid[:], pattern=[[1, SLOTS_R]], base=0, channel_multiplier=0).then_inc(s_const, 1)
            po.wait_ge(s_const, 10)
            po.tensor_copy(slotn[:], eid[:]).then_inc(s_const, 1)
            po.memset(slots[:, :, 0], TOK).then_inc(r_init, 1)
            po.memset(slots[:, :, 1], 0).then_inc(r_init, 1)
            po.memset(zrow, 0.0).then_inc(r_init, 1)
            po.wait_ge(r_init, 3)
            po.dma_start(slot_d.rearrange("(s p) a -> p s a", p=P), slots[:]).then_inc(r_fill, 16)
            po.dma_start(rows_d[TOK:TOK + 1, :], zrow).then_inc(r_fill, 16)

            def masks(b, q0, q1):
                wait_apart(po, s_adj[q0 > 0], b * 16 + 16)
                for qt in range(q0, q1):
                    mf = maski[:, qt].bitcast(F32)
                    po.tensor_scalar(mf, maski[:, qt], 0.0, SHUT, ALU.is_equal, ALU.mult).then_inc(s_penal, 1)
                    po.wait_ge(s_penal, b * QT + qt + 1)
                    po.tensor_tensor(adjm[:, qt], mf, adjm[:, qt], ALU.add).then_inc(s_adjm, 1)

            def norm(b):
                wait_apart(po, s_mv, b * QT + QT)
                po.tensor_scalar(mv[:, :, 1], mv[:, :, 1], EPS, None, ALU.add).then_inc(s_eps, 1)
                po.wait_ge(s_eps, b + 1)
                po.tensor_tensor(rstd[:], mv[:, :, 1], minus_half[:], ALU.pow).then_inc(s_rstd, 1)

            po.wait_ge(s_half, 1)
            norm(0)
            po.wait_ge(s_mask, 16)
            masks(0, 0, QT // 2)
            masks(0, QT // 2, QT)
            with po.Fori(0, B - 1) as b:
                norm(b + 1)
                po.wait_ge(s_mask, b * 16 + 32)
                masks(b + 1, 0, QT // 2)
                masks(b + 1, QT // 2, QT)
            with po.Fori(0, NT // 2) as i:
                for u in range(2):
                    wait_apart(po, t_mv, i * 2 + u + 1)
                    po.tensor_scalar(mv2[:, u, 1:2], mv2[:, u, 1:2], EPS, None, ALU.add).then_inc(t_eps, 1)
                    po.wait_ge(t_eps, i * 2 + u + 1)
                    po.tensor_tensor(rstd2[:, u:u + 1], mv2[:, u, 1:2], minus_half[:, 0:1],
                                     ALU.pow).then_inc(t_rstd, 1)
            po.wait_ge(r_fill, 32)
            po.wait_ge(r_pair, 1)
            for t in range(NT):
                po.indirect_dma_start(slot_d, bass.IndirectOffsetOnAxis(ap=posi[:, t:t + 1], axis=0),
                                      pair[:, t], None).then_inc(r_scat, 16)
            po.wait_ge(r_slots, 16)
            po.wait_ge(t_out, 16 * NT)

            def gather(s, u):
                po.tensor_copy(gidx[:, u:u + 1], slots[:, ds(s, 1), 0]).then_inc(f_gi, 1)
                wait_apart(po, f_gi, s + 1)
                po.indirect_dma_start(rows[:, u], None, rows_d,
                                      bass.IndirectOffsetOnAxis(ap=gidx[:, u:u + 1], axis=0)
                                      ).then_inc(f_row[u], 16)

            def scatter(s, u):
                po.tensor_copy(sidx[:, u:u + 1], slots[:, ds(s, 1), 0]).then_inc(f_si, 1)
                wait_apart(po, f_si, s + 1)
                po.indirect_dma_start(out_v, bass.IndirectOffsetOnAxis(ap=sidx[:, u:u + 1], axis=0),
                                      orow[:, u], None, bounds_check=TOK - 1,
                                      oob_is_err=False).then_inc(f_sc[u], 16)

            def scattered(i, u):
                po.wait_ge(f_sc[u], i * 16 + 16)
                po.sem_inc(f_free, 1)

            for u in range(2):
                gather(u, u)
            with po.Fori(0, (SLOTS - 3) // 2) as i:
                for u in range(2):
                    po.wait_ge(f_out, i * 2 + u + 1)
                    gather(i * 2 + (u + 2), u)
                    scatter(i * 2 + u, u)
                    scattered(i, u)
            for s in range(SLOTS - 3, SLOTS):
                po.wait_ge(f_out, s + 1)
                if s + 2 < SLOTS:
                    gather(s + 2, s % 2)
                scatter(s, s % 2)
                scattered(s // 2, s % 2)

        @block.tensor
        def _(pe):
            def bank_free(b, k):
                if isinstance(b, int) and BATCH_USES * b + k < 2:
                    return
                pe.wait_ge(s_md[k % 2], half(b, k))

            pe.wait_ge(s_const, 3)
            pe.wait_ge(s_wraw, 64)
            for w in range(4):
                bank_free(0, w)
                for k in range(EC):
                    for m in range(EC):
                        mm = pe.transpose(sp_bank[w % 2][:, k * E + m * P:k * E + (m + 1) * P],
                                          wraw[:, w, m, k * P:(k + 1) * P], ident[:])
                mm.then_inc(s_m, 1)
            pe.wait_ge(s_small, 64)
            bank_free(0, 4)
            nr = X * FC + 2 * EC
            pe.transpose(sp_bank[0][:, 0:nr], rowsm, ident[0:nr, 0:nr]).then_inc(s_m, 1)
            bank_free(0, 5)
            for k in range(EC):
                mm = pe.transpose(sp_bank[1][:, k * X:(k + 1) * X], gate_r[:, k * P:(k + 1) * P],
                                  ident[0:X, 0:X])
            mm.then_inc(s_m, 1)

            def turn(b, i, src):
                for k in range(EC):
                    bank_free(b, SETUP_USES + i + k)
                    for t in range(QT):
                        mm = pe.transpose(sp_bank[k][:, t * P:(t + 1) * P], src[:, t, k * P:(k + 1) * P],
                                          ident[:])
                    mm.then_inc(s_m, 1)

            def project(b, i, w, src, m):
                bank_free(b, SETUP_USES + i)
                for k in range(EC):
                    mm = pe.matmul(sp_bank[i % 2][:], wT[:, w, k, m * P:(m + 1) * P], src[:, k],
                                   start=k == 0, stop=k == EC - 1)
                mm.then_inc(s_m, 1)

            def turned(b, i):
                for k in range(EC):
                    pe.wait_ge(s_md[k], half(b, SETUP_USES + i) + 1)

            def turn_x(b):
                pe.wait_ge(s_xn, b * QT + QT)
                turn(b, 0, xin)

            def turn_ctx(b):
                pe.wait_ge(s_ctx, b * 16 + 16)
                turn(b, 2, cin)

            def project_q(b, m):
                if m == 0:
                    turned(b, 0)
                project(b, 4 + m, 0, xT, m)

            def project_k(b, m):
                if m == 0:
                    turned(b, 2)
                project(b, 6 + m, 1, cT, m)

            def values(b):
                for i in range(2):
                    bank_free(b, SETUP_USES + 8 + i)
                    for t in range(2):
                        for k in range(EC):
                            mm = pe.matmul(sp_bank[i][:, t * E:(t + 1) * E],
                                           cT[:, k, (2 * i + t) * P:(2 * i + t + 1) * P], wT[:, 2, k],
                                           start=k == 0, stop=k == EC - 1)
                    mm.then_inc(s_m, 1)

            def scores(b, par, n):
                g, qt, q2, h, j = tile_of(n)
                if n >= NS:
                    pe.wait_ge(s_masked, b * TILES + (n - NS + 1))
                q = stack[:, par, 0, h, qt * P:(qt + 1) * P].rearrange("p o q -> p (o q)")
                k = stack[:, par, 1, h, :].rearrange("p o q -> p (o q)")
                pe.matmul(sc_bank[n % NS][:], q, k, start=True, stop=True).then_inc(s_score, 1)

            def transposes(b, n):
                pe.wait_ge(s_exp, b * TILES + n + 1)
                if n >= NTB:
                    if (n - NTB) % 8 in DVE_COPIES:
                        pe.wait_ge(s_cdve, b * dve_copies(TILES) + dve_copies(n - NTB + 1))
                    else:
                        pe.wait_ge(s_cact, b * act_copies(TILES) + act_copies(n - NTB + 1))
                for c in range(QT):
                    mm = pe.transpose(tr_bank[n % NTB][:, c * P:(c + 1) * P], prob[:, n % NB, c * P:(c + 1) * P],
                                      ident[:])
                mm.then_inc(s_trans, 1)

            def weigh(b, g):
                pe.wait_ge(s_cact, b * act_copies(TILES) + act_copies(TPG * (g + 1)))
                pe.wait_ge(s_cdve, b * dve_copies(TILES) + dve_copies(TPG * (g + 1)))
                if g >= 2:
                    pe.wait_ge(s_osb, b * GROUPS + (g - 1))
                hg = g % NG
                for c in range(QT):
                    for j in range(HG):
                        mm = pe.matmul(pv_bank[32 * j:32 * j + 32, (g % 2) * HALF:(g % 2 + 1) * HALF],
                                       vals[:, c, hg * HG + j, :], pt[:, g % 2, c, j, :],
                                       start=c == 0, stop=c == QT - 1)
                mm.then_inc(s_pv, 1)

            def attention(b, par, nxt):
                values(b)
                pe.wait_ge(s_stack, b * (32 * PAIRS) + 32 * PAIRS)
                for n in range(TILES + LP + 1):
                    if n < TILES:
                        scores(b, par, n)
                    if n == 1:
                        pe.wait_ge(s_v, b * 2 + 2)
                    if LT <= n < TILES + LT:
                        transposes(b, n - LT)
                    if n >= LP + TPG and (n - LP) % TPG == 0:
                        weigh(b, (n - LP) // TPG - 1)
                    if nxt is not None:
                        if n == 16:
                            turn_x(nxt)
                        if n == 18:
                            turn_ctx(nxt)
                        if n in (22, 25):
                            project_q(nxt, (n - 22) // 3)
                        if n in (28, 31):
                            project_k(nxt, (n - 28) // 3)
                pe.wait_ge(s_osb, b * GROUPS + GROUPS)

            turn_x(0)
            turn_ctx(0)
            for m in range(EC):
                project_q(0, m)
            for m in range(EC):
                project_k(0, m)
            with pe.Fori(0, B - 1) as b:
                attention(b, ds(b % 2, 1), b + 1)
            attention(B - 1, ds((B - 1) % 2, 1), None)

            with pe.Fori(0, NT // 2) as i:
                for u in range(2):
                    pe.wait_ge(t_oc, i * 2 + u + 1)
                    for a in range(NG):
                        mm = pe.transpose(bank[4 * u][:, a * P:(a + 1) * P], oc[:, u, a], ident[:])
                    mm.then_inc(t_ot, 1)
                for u in range(2):
                    pe.wait_ge(t_attn, i * 2 + u + 1)
                    for k in range(EC):
                        mm = pe.transpose(bank[4 * u + 1][:, k * P:(k + 1) * P], attn[:, u, k * P:(k + 1) * P],
                                          ident[:])
                    mm.then_inc(t_at, 1)
                for u in range(2):
                    pe.wait_ge(t_atT, i * 2 + u + 1)
                    for k in range(EC):
                        mm = pe.matmul(bank[4 * u + 2][:, 0:E], atT[:, u, k], wT[:, 3, k],
                                       start=k == 0, stop=k == EC - 1)
                    mm.then_inc(t_op, 1)
                for u in range(2):
                    pe.wait_ge(t_row, i * 2 + u + 1)
                    for k in range(EC):
                        mm = pe.transpose(bank[4 * u + 1][:, E + k * P:E + (k + 1) * P],
                                          rows[:, u, E + k * P:E + (k + 1) * P], ident[:])
                    mm.then_inc(t_x2, 1)
                for u in range(2):
                    pe.wait_ge(t_x2T, i * 2 + u + 1)
                    for k in range(EC):
                        mm = pe.matmul(bank[4 * u + 3][:, 0:X], x2T[:, u, k], gateT[:, k],
                                       start=k == 0, stop=k == EC - 1)
                    mm.then_inc(t_lg, 1)

            pe.wait_ge(r_oh, 1)
            oh = rt_flat[:, 0:NT * X]
            pe.matmul(bank[0][:, 0:NT * X], ltri[:], oh, start=True, stop=True)
            pe.matmul(bank[1][:, 0:NT * X], ones[:], oh, start=True, stop=True).then_inc(r_rank, 1)

            def expert(s, i, u):
                e = pe.value_load(eid[0:1, ds(s, 1)], min_val=0, max_val=X - 1)
                pe.wait_ge(f_row[u], i * 16 + 16)
                for k in range(EC):
                    mm = pe.transpose(bank[4 * u][:, k * P:(k + 1) * P], rows[:, u, E + k * P:E + (k + 1) * P],
                                      ident[:])
                mm.then_inc(f_xt, 1)
                pe.wait_ge(f_w1[u], i * 16 + 16)
                pe.wait_ge(f_xgT, s + 1)
                for c in range(FC):
                    o = bank[4 * u + 1 + c // 4][:, (c % 4) * P:(c % 4 + 1) * P]
                    for k in range(EC):
                        mm = pe.matmul(o, w1s[:, u, k, c * P:(c + 1) * P], xgT[:, u, k],
                                       start=k == 0, stop=k == EC - 1)
                    mm.then_inc(f_h, 1)
                for c in range(FC):
                    pe.wait_ge(f_hT, s * FC + c + 1)
                    mm = pe.matmul(bank[4 * u + 3][:, 0:E], hT[:, u, c],
                                   w2s[:, ds(e, 1), c, :].rearrange("p x e -> p (x e)"),
                                   start=c == 0, stop=c == FC - 1)
                mm.then_inc(f_y, 1)

            pe.wait_ge(r_eid, 1)
            pe.wait_ge(r_w2, 16 * X)
            with pe.Fori(0, SLOTS // 2) as i:
                for u in range(2):
                    expert(i * 2 + u, i, u)
            expert(SLOTS - 1, SLOTS // 2, 0)

        @block.scalar
        def _(act):
            for w in range(4):
                act.wait_ge(s_m, w + 1)
                act.activation(wT[:, w], sp_bank[w % 2][:].rearrange("p (k f) -> p k f", k=EC), ACT.Copy,
                               scale=float(D) ** -0.5 if w == 0 else 1.0).then_inc(s_md[w % 2], 1)
            act.wait_ge(s_m, 5)
            act.activation(colsm[:], sp_bank[0][:, 0:X * FC + 2 * EC], ACT.Copy).then_inc(s_tg, 1)
            act.wait_ge(s_tg, 1)
            act.activation(bqc, bqc, ACT.Copy, scale=float(D) ** -0.5).then_inc(s_md[0], 1)
            act.wait_ge(s_m, 6)
            act.activation(gateT[:].rearrange("p k x -> p (k x)"), sp_bank[1][:, 0:EC * X],
                           ACT.Copy).then_inc(s_md[1], 1)
            act.wait_ge(s_bcast, 64)
            act.activation(tg[:], gr[:], ACT.Tanh).then_inc(s_tg, 1)
            act.wait_ge(s_md[0], 3)

            def copy_turned(b, i, dst):
                for k in range(EC):
                    act.wait_ge(s_m, pro_use(b, i + k) + 1)
                    act.activation(dst[:, k], sp_bank[k][:], ACT.Copy).then_inc(s_md[k], 1)

            def first_part(b, t, m):
                i = 4 + 2 * t + m
                act.wait_ge(s_m, pro_use(b, i) + 1)
                if not (isinstance(b, int) and b == 0):
                    act.wait_ge(s_partd[t], b * 32)
                act.activation(parts[:, t, m, 0], sp_bank[i % 2][:], ACT.Identity,
                               bias=(bqc, bkc)[t][:, m:m + 1]).then_inc(s_p0, 1)

            def attention(b, nxt):
                for n in range(TILES + LE):
                    c = n - LE
                    if c >= 0 and c % 8 not in DVE_COPIES:
                        g, qt, q2, h, j = tile_of(c)
                        act.wait_ge(s_trans, b * TILES + c + 1)
                        if g >= 2:
                            act.wait_ge(s_pv, b * GROUPS + (g - 1))
                        act.activation(pt[:, g % 2, :, j, q2 * P:(q2 + 1) * P],
                                       tr_bank[c % NTB][:].rearrange("p (c q) -> p c q", c=QT),
                                       ACT.Copy).then_inc(s_cact, 1)
                    if n < TILES:
                        act.wait_ge(s_masked, b * TILES + n + 1)
                        act.activation(prob[:, n % NB], prob[:, n % NB], ACT.Exp, scale=-1.0,
                                       bias=negmax[:, n % NB:n % NB + 1]).then_inc(s_exp, 1)
                    if nxt is not None:
                        if n == 17:
                            copy_turned(nxt, 0, xT)
                        if n == 19:
                            copy_turned(nxt, 2, cT)
                        if n in (23, 26, 29, 32):
                            first_part(nxt, (n - 23) // 6, (n - 23) // 3 % 2)
                act.wait_ge(s_pv, b * GROUPS + GROUPS)

            copy_turned(0, 0, xT)
            copy_turned(0, 2, cT)
            for t in range(2):
                for m in range(EC):
                    first_part(0, t, m)
            with act.Fori(0, B - 1) as b:
                attention(b, b + 1)
            attention(B - 1, None)

            act.wait_ge(s_osb, B * GROUPS)
            with act.Fori(0, NT // 2) as i:
                for u in range(2):
                    act.activation(oc[:, u], o_sb[:, :, ds(i * 2 * P + u * P, P)], ACT.Copy).then_inc(t_oc, 1)
                for u in range(2):
                    act.wait_ge(t_at, i * 2 + u + 1)
                    act.activation(atT[:, u], bank[4 * u + 1][:, 0:E].rearrange("p (k q) -> p k q", k=EC),
                                   ACT.Copy).then_inc(t_atT, 1)
                for u in range(2):
                    act.wait_ge(t_x2, i * 2 + u + 1)
                    act.activation(x2T[:, u], bank[4 * u + 1][:, E:2 * E].rearrange("p (k q) -> p k q", k=EC),
                                   ACT.Copy).then_inc(t_x2T, 1)
                for u in range(2):
                    act.wait_ge(t_lg, i * 2 + u + 1)
                    act.activation(logit[:, ds(i * 2 + u, 1), :].rearrange("p t x -> p (t x)"),
                                   bank[4 * u + 3][:, 0:X], ACT.Copy).then_inc(t_logit, 1)
            act.wait_ge(r_sub, 1)
            act.activation(logit[:], logit[:], ACT.Exp).then_inc(r_exp, 1)

            def expert(s, i, u):
                e = act.value_load(eid[0:1, ds(s, 1)], min_val=0, max_val=X - 1)
                act.wait_ge(f_xt, s + 1)
                act.activation(xgT[:, u], bank[4 * u][:, 0:E].rearrange("p (k q) -> p k q", k=EC),
                               ACT.Copy).then_inc(f_xgT, 1)
                for c in range(FC):
                    if c % 4 == 0:
                        act.wait_ge(f_h, s * FC + c + 4)
                    act.activation(hT[:, u, c], bank[4 * u + 1 + c // 4][:, (c % 4) * P:(c % 4 + 1) * P],
                                   ACT.Relu, bias=b1c[:, ds(e * FC + c, 1)]).then_inc(f_hT, 1)

            act.wait_ge(r_eid, 1)
            with act.Fori(0, SLOTS // 2) as i:
                for u in range(2):
                    expert(i * 2 + u, i, u)
            expert(SLOTS - 1, SLOTS // 2, 0)

        @block.vector
        def _(ve):
            ve.wait_ge(s_tg, 2)

            def norm_stats(b):
                ve.wait_ge(s_x, b * 16 + 16)
                for t in range(QT):
                    ve.bn_stats(stats[:, t], xin[:, t]).then_inc(s_stat, 1)
                for t in range(QT):
                    wait_apart(ve, s_stat, b * QT + t + 1)
                    ve.bn_aggr(mv[:, t], stats[:, t]).then_inc(s_mv, 1)

            def norm(b):
                ve.wait_ge(s_rstd, b + 1)
                for t in range(QT):
                    ve.tensor_scalar(xin[:, t], xin[:, t], mv[:, t, 0:1], rstd[:, t:t + 1],
                                     ALU.subtract, ALU.mult).then_inc(s_xn, 1)

            def other_parts(b, t, m):
                i = 4 + 2 * t + m
                k = 2 * t + m + 1
                ve.wait_ge(s_p0, b * 4 + k)
                if not isinstance(b, int) or k > 1:
                    ve.wait_ge(s_parts, b * 4 + (k - 1))
                ve.scalar_tensor_tensor(out=rest[:], in0=sp_bank[i % 2][:], scalar=(bqc, bkc)[t][:, m:m + 1],
                                        in1=parts[:, t, m, 0], op0=ALU.add, op1=ALU.subtract
                                        ).then_inc(s_md[i % 2], 1)
                ve.wait_ge(s_md[i % 2], half(b, SETUP_USES + i) + 1)
                ve.tensor_copy(parts[:, t, m, 1], rest[:]).then_inc(s_p1, 1)
                ve.wait_ge(s_p1, b * 4 + k)
                ve.tensor_tensor(parts[:, t, m, 2], rest[:], parts[:, t, m, 1], ALU.subtract).then_inc(s_parts, 1)

            def values(b):
                for i in range(2):
                    ve.wait_ge(s_m, val_use(b, i) + 1)
                    for t in range(2):
                        ins = ve.tensor_tensor(vals[:, 2 * i + t, :, 0:D],
                                               sp_bank[i][:, t * E:(t + 1) * E].rearrange("p (h d) -> p h d", d=D),
                                               bvb[:].rearrange("p (h d) -> p h d", d=D), ALU.add)
                        if t == 0:
                            ins.then_inc(s_rest, 1)
                    ins.then_inc(s_v, 1)
                    ve.wait_ge(s_v, b * 2 + i + 1)
                    ve.wait_ge(s_rest, b * 2 + i + 1)
                    ve.sem_inc(s_md[i], 1)

            def attention(b, nxt):
                values(b)
                for n in range(TILES + LP + 1):
                    c = n - LE
                    if 0 <= c < TILES and c % 8 in DVE_COPIES:
                        g, qt, q2, h, j = tile_of(c)
                        ve.wait_ge(s_trans, b * TILES + c + 1)
                        if g >= 2:
                            ve.wait_ge(s_pv, b * GROUPS + (g - 1))
                        ve.tensor_copy(pt[:, g % 2, :, j, q2 * P:(q2 + 1) * P],
                                       tr_bank[c % NTB][:].rearrange("p (c q) -> p c q", c=QT)).then_inc(s_cdve, 1)
                    if n < TILES:
                        g, qt, q2, h, j = tile_of(n)
                        if n % (TILES // 2) == 0:
                            ve.wait_ge(s_adjm, b * QT + (qt + QT // 2))
                        if n >= NB:
                            ve.wait_ge(s_trans, b * TILES + (n - NB + 1))
                        wait_apart(ve, s_score, b * TILES + n + 1)
                        ve.tensor_tensor_reduce(out=prob[:, n % NB], in0=sc_bank[n % NS][:], in1=adjm[:, qt],
                                                scale=-1.0, scalar=BIG, op0=ALU.add, op1=ALU.min,
                                                accum_out=negmax[:, n % NB:n % NB + 1]).then_inc(s_masked, 1)
                    if n >= LP + TPG and (n - LP) % TPG == 0:
                        g = (n - LP) // TPG - 1
                        ve.wait_ge(s_pv, b * GROUPS + g + 1)
                        ve.tensor_copy(o_sb[:, g % NG, ds(b * S + (g // NG) * HALF, HALF)],
                                       pv_bank[:, (g % 2) * HALF:(g % 2 + 1) * HALF]).then_inc(s_osb, 1)
                    if nxt is not None:
                        if n == 8:
                            norm_stats(nxt)
                        if n == 12:
                            norm(nxt)
                        if n in (24, 27, 30, 33):
                            other_parts(nxt, (n - 24) // 6, (n - 24) // 3 % 2)
                ve.wait_ge(s_trans, b * TILES + TILES)

            norm_stats(0)
            norm(0)
            for t in range(2):
                for m in range(EC):
                    other_parts(0, t, m)
            ve.wait_ge(s_bcast, 64)
            ve.wait_ge(s_vinit, 2)
            ve.wait_ge(r_fill, 32)
            with ve.Fori(0, B - 1) as b:
                attention(b, b + 1)
            attention(B - 1, None)

            ve.sem_inc(t_x1, 2)
            ve.wait_ge(s_const, 11)
            with ve.Fori(0, NT // 2) as i:
                for u in range(2):
                    o4 = bank[4 * u][:].rearrange("p (h w) -> p h w", w=VW)
                    ve.wait_ge(t_ot, i * 2 + u + 1)
                    ve.reciprocal(rinv[:, u], o4[:, :, D]).then_inc(t_rinv, 1)
                    ve.wait_ge(t_rinv, i * 2 + u + 1)
                    ve.tensor_tensor(attn[:, u].rearrange("p (h d) -> p h d", d=D), o4[:, :, 0:D],
                                     rinv[:, u].rearrange("p (h o) -> p h o", o=1).to_broadcast([P, H, D]),
                                     ALU.mult).then_inc(t_attn, 1)
                for u in range(2):
                    r = rows[:, u]
                    ve.wait_ge(t_op, i * 2 + u + 1)
                    ve.wait_ge(t_x[u], i * 16 + 16)
                    ve.tensor_tensor(r[:, 0:E], bank[4 * u + 2][:, 0:E], bob[:], ALU.add).then_inc(t_y, 1)
                    ve.wait_ge(t_y, i * 2 + u + 1)
                    ve.scalar_tensor_tensor(out=r[:, 0:E], in0=r[:, 0:E], scalar=tg[:, 0:1], in1=xres[:, u],
                                            op0=ALU.mult, op1=ALU.add).then_inc(t_x1, 1)
                    ve.wait_ge(t_x1, i * 2 + u + 3)
                    ve.bn_stats(st2[:, u], r[:, 0:E]).then_inc(t_stat, 1)
                    wait_apart(ve, t_stat, i * 2 + u + 1)
                    ve.bn_aggr(mv2[:, u], st2[:, u]).then_inc(t_mv, 1)
                for u in range(2):
                    r = rows[:, u]
                    ve.wait_ge(t_rstd, i * 2 + u + 1)
                    ve.tensor_scalar(r[:, E:2 * E], r[:, 0:E], mv2[:, u, 0:1], rstd2[:, u:u + 1],
                                     ALU.subtract, ALU.mult).then_inc(t_row, 1)
                ve.wait_ge(t_out, i * 32 + 32)

            done = 0

            def link(ins):
                nonlocal done
                done += 1
                ins.then_inc(r_dve, 1)
                ve.wait_ge(r_dve, done)

            n8 = NT * X

            def buf(k, w=n8):
                return rt_flat[:, k * n8:k * n8 + w]

            def by_tile(ap):
                return ap.rearrange("p (t x) -> p t x", x=X)

            def per_tile(ap):
                return ap.rearrange("p (t o) -> p t o", o=1).to_broadcast([P, NT, X])

            def per_expert(ap):
                return ap.rearrange("p (o x) -> p o x", o=1).to_broadcast([P, NT, X])

            oh, key, cum, cum2, tmp = (buf(k) for k in range(5))
            small = rt_flat[:, 5 * n8:]
            mx, sm, em, km, wt, posf = (small[:, k * NT:(k + 1) * NT] for k in range(6))
            cnt, end, end2, first = (small[:, 128 + k * X:128 + (k + 1) * X] for k in range(4))
            ef = small[:, 192:192 + SLOTS_R]
            cmp = small[:, 256:256 + SLOTS_R * X]

            ve.wait_ge(t_logit, NT)
            link(ve.tensor_reduce(mx, logit[:], AX.X, ALU.max))
            ve.tensor_tensor(logit[:], logit[:], per_tile(mx), ALU.subtract).then_inc(r_sub, 1)
            ve.wait_ge(r_exp, 1)
            link(ve.tensor_reduce(sm, logit[:], AX.X, ALU.add))
            link(ve.tensor_reduce(em, logit[:], AX.X, ALU.max))
            link(ve.tensor_tensor(by_tile(key), logit[:], per_tile(em), ALU.is_equal))
            link(ve.tensor_tensor(by_tile(key), by_tile(key), per_expert(seven[:]), ALU.mult))
            link(ve.tensor_reduce(km, by_tile(key), AX.X, ALU.max))
            ve.tensor_tensor(by_tile(oh), by_tile(key), per_tile(km), ALU.is_equal).then_inc(r_oh, 1)
            link(ve.reciprocal(wt, sm))
            link(ve.tensor_tensor(wt, wt, em, ALU.mult))
            link(ve.tensor_scalar(pair[:].bitcast(F32)[:, :, 1], wt, tg[:, 1:2], None, ALU.mult))
            ve.wait_ge(r_rank, 1)
            link(ve.tensor_copy(cum, bank[1][:, 0:n8]))
            src, dst = cum, cum2
            step = 1
            while step < NT:
                w = step * X
                ve.tensor_copy(dst[:, 0:w], src[:, 0:w])
                link(ve.tensor_tensor(dst[:, w:], src[:, w:], src[:, 0:n8 - w], ALU.add))
                src, dst = dst, src
                step *= 2
            link(ve.tensor_tensor(tmp[:, X:], bank[0][:, X:n8], src[:, 0:n8 - X], ALU.add))
            link(ve.tensor_copy(tmp[:, 0:X], bank[0][:, 0:X]))
            link(ve.tensor_copy(cnt, src[:, n8 - X:]))
            link(ve.tensor_tensor(key.rearrange("p (x t) -> p x t", x=X),
                                  cnt.rearrange("p (x o) -> p x o", o=1).to_broadcast([P, X, NT]),
                                  thr[:].rearrange("p (o t) -> p o t", o=1).to_broadcast([P, X, NT]), ALU.is_gt))
            link(ve.tensor_reduce(first, key.rearrange("p (x t) -> p x t", x=X), AX.X, ALU.add))
            link(ve.tensor_copy(end, first))
            a, z = end, end2
            step = 1
            while step < X:
                ve.tensor_copy(z[:, 0:step], a[:, 0:step])
                link(ve.tensor_tensor(z[:, step:], a[:, step:], a[:, 0:X - step], ALU.add))
                a, z = z, a
                step *= 2
            link(ve.tensor_tensor(first, a, first, ALU.subtract))
            link(ve.tensor_scalar(first, first, float(P), None, ALU.mult))
            link(ve.tensor_tensor(by_tile(tmp), by_tile(tmp), per_expert(first), ALU.add))
            link(ve.tensor_tensor(tmp, tmp, oh, ALU.mult))
            link(ve.tensor_reduce(posf, by_tile(tmp), AX.X, ALU.add))
            ve.tensor_copy(posi[:], posf).then_inc(r_pair, 1)
            cmp3 = cmp.rearrange("p (s x) -> p s x", x=X)
            link(ve.tensor_tensor(cmp3, slotn[:].rearrange("p (s o) -> p s o", o=1).to_broadcast([P, SLOTS_R, X]),
                                  a.rearrange("p (o x) -> p o x", o=1).to_broadcast([P, SLOTS_R, X]), ALU.is_ge))
            link(ve.tensor_reduce(ef, cmp3, AX.X, ALU.add))
            ve.tensor_scalar(eid[:], ef, float(X - 1), None, ALU.min).then_inc(r_eid, 1)

            def expert(s, i, u):
                e = ve.value_load(eid[0:1, ds(s, 1)], min_val=0, max_val=X - 1)
                ve.wait_ge(f_y, s + 1)
                ve.tensor_tensor(ytmp[:, u], bank[4 * u + 3][:, 0:E],
                                 b2b[:, ds(e, 1), :].rearrange("p x e -> p (x e)"), ALU.add).then_inc(f_tmp, 1)
                ve.wait_ge(f_tmp, s + 1)
                ve.wait_ge(f_free, s + 1)
                ve.scalar_tensor_tensor(out=orow[:, u], in0=ytmp[:, u],
                                        scalar=slots[:].bitcast(F32)[:, ds(s, 1), 1], in1=rows[:, u, 0:E],
                                        op0=ALU.mult, op1=ALU.add).then_inc(f_out, 1)

            ve.sem_inc(f_free, 2)
            ve.wait_ge(r_eid, 1)
            ve.wait_ge(r_slots, 16)
            ve.wait_ge(r_b2, 16)
            with ve.Fori(0, SLOTS // 2) as i:
                for u in range(2):
                    expert(i * 2 + u, i, u)
            expert(SLOTS - 1, SLOTS // 2, 0)


_INS = ["x", "ctx_1024", "mask_Bx1xSxS2_ik1", "g_xattn", "g_ffn", "L0_xattn_adj", "L0_xattn_Wq",
        "L0_xattn_bq", "L0_xattn_Wk", "L0_xattn_bk", "L0_xattn_Wv", "L0_xattn_bv", "L0_xattn_Wo",
        "L0_xattn_bo", "L0_ffn_gate_w", "L0_ffn_w1", "L0_ffn_b1", "L0_ffn_w2", "L0_ffn_b2"]


def kernel(**inputs):
    import numpy as np
    import concourse.bacc as bacc
    from concourse.bass_utils import run_bass_kernel_spmd

    nc = bacc.Bacc("TRN2", target_bir_lowering=False, num_devices=1)
    arrays, args = {}, []
    for name in _INS:
        a = np.ascontiguousarray(inputs[name])
        arrays[f"in_{name}"] = a
        args.append(nc.dram_tensor(f"in_{name}", a.shape, mybir.dt.from_np(a.dtype), kind="ExternalInput").ap())
    shape = inputs["x"].shape
    out = nc.dram_tensor("out_y", shape, F32, kind="ExternalOutput").ap()
    build(nc, *args, out)
    r = run_bass_kernel_spmd(nc, [arrays], core_ids=[0])
    return r.results[0]["out_y"]
```

```python
from contextlib import ExitStack

import concourse.bass as bass
from concourse import mybir

ALU = mybir.AluOpType
ACT = mybir.ActivationFunctionType
AX = mybir.AxisListType
F32 = mybir.dt.float32
BF16 = mybir.dt.bfloat16
I32 = mybir.dt.int32
ds = bass.ds

P = 128
EPS = 1e-5
SHUT = -1e30
BIG = 3e38

Q_PART = [0, 0, 1, 1, 0, 2, 1, 2]
K_PART = [0, 1, 0, 1, 2, 0, 2, 1]
PAIRS = len(Q_PART)


def build(nc, x, ctx_in, mask, g_xattn, g_ffn, adj, Wq, bq, Wk, bk, Wv, bv, Wo, bo,
          gate_w, w1, b1, w2, b2, out):
    B, S, E = x.shape
    X, _, DFF = w1.shape
    D = P // PAIRS
    H = E // D
    QT = S // P
    EC = E // P
    FC = DFF // P
    TOK = B * S
    NT = TOK // P
    SLOTS = NT + X - 1
    SLOTS_R = SLOTS + SLOTS % 2
    HG = 4
    NG = H // HG
    QH = 2
    GROUPS = QH * NG
    QPG = QT // QH
    TPG = QPG * HG
    TILES = GROUPS * TPG
    HALF = S // QH
    VW = 32
    assert (D, H, E, S) == (16, 16, 256, 512)

    NB = 6
    NS = 3
    NTB = 2
    LT = 4
    LE = 4
    LP = LE + 1
    DVE_COPIES = (1, 4, 6)

    def dve_copies(n):
        return sum(1 for i in range(n) if i % 8 in DVE_COPIES)

    def act_copies(n):
        return n - dve_copies(n)

    SETUP = 6
    NEXT = 8
    TAIL_A = [(2, "heads", 0), (3, "heads", 1), (5, "turn", 0), (6, "turn", 1), (8, "out", 0),
              (9, "out", 1), (14, "normed", 0), (15, "normed", 1), (17, "gate", (0, 1)), (22, "rank", 0)]
    USES = ([(0, "values", 0), (1, "values", 1)] + TAIL_A
            + [(24, "next x", 0), (25, "next x", 1), (26, "next ctx", 0), (27, "next ctx", 1),
               (29, "next q", 0), (31, "next q", 1), (33, "next k", 0), (35, "next k", 1)]
            + [(39, "heads", 2), (40, "heads", 3), (42, "turn", 2), (43, "turn", 3), (45, "out", 2),
               (46, "out", 3), (51, "normed", 2), (52, "normed", 3), (54, "gate", (2,)), (55, "gate", (3,))])
    LAST_USES = [u for u in USES if not u[1].startswith("next")]
    NEXT_USES = [(k, w, a) for k, w, a in USES if w.startswith("next")]
    ROW_STEPS = {12: 0, 13: 1, 49: 2, 50: 3}
    PER = len(USES)
    LAST_SHIFT = len(LAST_USES) - PER
    assert PER % 2 == 0 and len(NEXT_USES) == NEXT

    def at_step(uses, n):
        return [(i, w, a) for i, (k, w, a) in enumerate(uses) if k == n]

    def ready(b, i):
        return b * PER + (SETUP + NEXT + i + 1)

    def free(b, i):
        return b * (PER // 2) + (SETUP + NEXT + i) // 2

    with ExitStack() as st:
        def sb(name, shape, dt=F32):
            return st.enter_context(nc.sbuf_tensor(name, shape, dt))

        def sem(name):
            return st.enter_context(nc.semaphore(name))

        w2s = sb("w2s", [P, X, FC, E])
        stack = w2s[:].rearrange("p x c e -> p (x c e)").bitcast(BF16).rearrange(
            "p (b t h s) -> p b t h s", b=2, t=2, h=H)
        pt = sb("pt", [P, 2, QT, HG, HALF])
        pt_flat = pt[:].rearrange("p a c j q -> p (a c j q)")
        wraw = pt_flat[:, 0:4 * EC * E].rearrange("p (w m e) -> p w m e", w=4, m=EC)
        w1s = pt_flat.rearrange("p (u k f) -> p u k f", u=4, k=EC)
        prob = sb("prob", [P, NB, S])
        negmax = sb("negmax", [P, NB])
        vals = sb("vals", [P, QT, H, VW])
        o_sb = sb("o_sb", [P, NG, QH, HALF])
        adjm = sb("adjm", [P, QT, S])
        maski = sb("maski", [P, QT, S], I32)
        xin = sb("xin", [P, QT, E])
        cin = sb("cin", [P, QT, E])
        xT = sb("xT", [P, EC, S])
        cT = sb("cT", [P, EC, S])
        parts = sb("parts", [P, 2, EC, 3, S], BF16)
        rest = sb("rest", [P, S])
        wT = sb("wT", [P, 4, EC, E])
        minus_half = sb("minus_half", [P, QT])
        ident = sb("ident", [P, P])
        stats = sb("stats", [P, QT, 6])
        mv = sb("mv", [P, QT, 2])
        rstd = sb("rstd", [P, QT])
        early = prob[:].rearrange("p n s -> p (n s)")
        zrow = early[0:1, 0:2 * E]
        gate_r = early[0:X, 2 * E:3 * E]
        rowsm = early[0:X * FC + 2 * EC, 3 * E:3 * E + P]
        colsm = sb("colsm", [P, X * FC + 4])
        gateT = sb("gateT", [P, EC, X])
        bvb = sb("bvb", [P, E])
        bob = sb("bob", [P, E])
        gr = sb("gr", [P, 2])
        tg = sb("tg", [P, 2])
        logit = sb("logit", [P, QT, X])
        b1c = colsm[:, 0:X * FC]
        bqc = colsm[:, X * FC:X * FC + EC]
        bkc = colsm[:, X * FC + EC:X * FC + 2 * EC]
        rows = sb("rows", [P, 2, 2 * E])
        xres = sb("xres", [P, 2, E])
        attn = sb("attn", [P, 2, E])
        atT = sb("atT", [P, 2, EC, P])
        x2T = sb("x2T", [P, 2, EC, P])
        b2b = maski[:].rearrange("p t s -> p (t s)").bitcast(F32).rearrange("p (x e) -> p x e", x=X)
        hT = adjm[:].rearrange("p t s -> p (t s)").rearrange("p (u c t) -> p u c t", u=2, c=FC)
        xgT = xT[:].rearrange("p k (u t) -> p u k t", u=4)[:, 0:2]
        orow = cT[:, 0].rearrange("p (u e) -> p u e", u=2)
        ytmp = cT[:, 1].rearrange("p (u e) -> p u e", u=2)
        rinv = sb("rinv", [P, 2, H])
        st2 = sb("st2", [P, 2, 6])
        mv2 = sb("mv2", [P, 2, 2])
        rstd2 = sb("rstd2", [P, 2])
        ids = sb("ids", [P, B + 1, QT], I32)
        pair = sb("pair", [P, QT, 2], I32)
        posi = sb("posi", [P, QT], I32)
        empty = sb("empty", [P, TOK * X // P, 2], I32)
        slots = sb("slots", [P, SLOTS_R, 2], I32)
        eid = sb("eid", [P, SLOTS_R], I32)
        base_i = sb("base_i", [P, SLOTS_R], I32)
        gidx = sb("gidx", [P, 2], I32)
        sidx = sb("sidx", [P, 2], I32)
        ltri = sb("ltri", [P, P], BF16)
        ones = sb("ones", [P, P], BF16)
        onehot = sb("onehot", [P, QT, X], BF16)
        seven = sb("seven", [P, X])
        region = sb("region", [P, X])
        region0 = sb("region0", [P, X])
        thr = sb("thr", [P, NT])
        slotn = sb("slotn", [P, SLOTS_R])
        live = sb("live", [P, B + 1])
        dead = sb("dead", [P, B + 1])
        iot = sb("iot", [P, SLOTS_R], I32)
        key, place = (sb(n, [P, QT, X]) for n in ("key", "place"))
        mx, sm, em, km, wt, posf = (sb(n, [P, QT]) for n in ("mx", "sm", "em", "km", "wt", "posf"))
        cnt, tiles, end, end2, span = (sb(n, [P, X]) for n in ("cnt", "tiles", "end", "end2", "span"))
        cmp_t = sb("cmp_t", [P, X, NT])
        cmp_s = sb("cmp_s", [P, SLOTS_R, X])
        ef, bf = sb("ef", [P, SLOTS_R]), sb("bf", [P, SLOTS_R])

        bank = [st.enter_context(nc.psum_tensor(f"bank{i}", [P, 512], F32)) for i in range(8)]
        sc_bank, tr_bank, pv_bank, sp_bank = bank[0:NS], bank[NS:NS + NTB], bank[5], bank[6:8]

        part_d = nc.dram_tensor("part_d", [2, 2, 3, E, S], BF16, kind="Internal").ap()
        rows_d = nc.dram_tensor("rows_d", [TOK + 1, 2 * E], F32, kind="Internal").ap()
        slot_d = nc.dram_tensor("slot_d", [X * TOK + P, 2], I32, kind="Internal").ap()

        x_v = x.rearrange("b (t p) e -> b p t e", p=P)
        c_v = ctx_in.rearrange("b (t p) e -> b p t e", p=P)
        m_v = mask.rearrange("b o (t p) s -> b p (o t) s", p=P)
        adj_v = adj.rearrange("(t p) s -> p t s", p=P)
        xt_v = x.rearrange("b (t p) e -> (b t) p e", p=P)
        out_v = out.rearrange("b s e -> (b s) e")
        w1_v = w1.rearrange("x (k p) f -> x p k f", p=P)

        (s_wraw, s_small, s_bcast, s_x, s_ctx, s_mask, s_const, s_m, s_stat, s_mv, s_rstd,
         s_xn, s_p0, s_rest, s_p1, s_parts, s_stack, s_adjm, s_penal, s_v, s_score,
         s_xT, s_masked, s_exp, s_trans, s_cact, s_cdve, s_pv, s_osb, s_tg, s_vinit) = [
            sem(n) for n in (
                "wraw", "small", "bcast", "x", "ctx", "mask", "const", "m", "stat", "mv",
                "rstd", "xn", "p0", "rest", "p1", "parts", "stack", "adjm", "penal", "v",
                "score", "xT", "masked", "exp", "trans", "cact", "cdve", "pv", "osb", "tg", "vinit")]
        s_waited = [sem("waited0"), sem("waited1")]
        s_partd, s_adj, t_x, t_out = ([sem(f"{n}{k}") for k in range(2)]
                                      for n in ("partd", "adj", "t_xres", "t_out"))
        r_fill, f_free = sem("r_fill"), sem("f_free")
        s_eps, t_eps, s_half = sem("eps"), sem("t_eps"), sem("half")
        s_md = [sem("md0"), sem("md1")]
        (t_rinv, t_attn, t_atT, t_x1, t_stat, t_mv, t_rstd, t_row, t_x2T, t_rowfree, r_dve, t_ones) = [
            sem("t_" + n) for n in (
                "rinv", "attn", "atT", "x1", "stat", "mv", "rstd", "row", "x2T", "rowfree", "r_dve", "ones")]
        (r_exp, r_sub, r_oh, r_pair, r_scat, r_free, r_ids, r_init, r_eid, r_w2,
         r_b2, r_mx, r_st, r_wt) = [sem("r_" + n) for n in (
             "exp", "sub", "oh", "pair", "scat", "free", "ids", "init", "eid",
             "w2", "b2", "mx", "st", "wt")]
        r_slots = [sem("r_slots0"), sem("r_slots1")]
        (f_xt, f_xgT, f_h, f_hT, f_y, f_tmp, f_out, f_gi, f_si) = [
            sem("f_" + n) for n in ("xt", "xgT", "h", "hT", "y", "tmp", "out", "gi", "si")]
        f_w1 = [sem("f_w1_0"), sem("f_w1_1")]
        f_row = [sem("f_row0"), sem("f_row1")]
        f_sc = [sem("f_sc0"), sem("f_sc1")]

        block = st.enter_context(nc.Block())

        def wait_apart(eng, s, value):
            eng.wait_ge(s, value)
            eng.sem_inc(s_waited[eng is nc.vector], 1)

        def tile_of(n):
            g, r = divmod(n, TPG)
            qh, hg = divmod(g, NG)
            q2, j = divmod(r, HG)
            return g, qh * QPG + q2, q2, hg * HG + j, j

        @block.sync
        def _(sp):
            for n, w in enumerate((Wq, Wk, Wv, Wo)):
                sp.dma_start(wraw[:, n], w.rearrange("(m p) e -> p m e", p=P)).then_inc(s_wraw, 16)
            sp.dma_start(xin[:], x_v[0]).then_inc(s_x, 16)
            sp.dma_start(cin[:], c_v[0]).then_inc(s_ctx, 16)
            sp.dma_start(rowsm[0:X * FC, :], b1.rearrange("x (c p) -> (x c) p", p=P)).then_inc(s_small, 16)
            sp.dma_start(rowsm[X * FC:X * FC + EC, :], bq.rearrange("(c p) -> c p", p=P)).then_inc(s_small, 16)
            sp.dma_start(rowsm[X * FC + EC:X * FC + 2 * EC, :], bk.rearrange("(c p) -> c p", p=P)).then_inc(s_small, 16)
            sp.dma_start(gate_r, gate_w).then_inc(s_small, 16)
            sp.dma_start(maski[:], m_v[0]).then_inc(s_mask, 16)

            def load_adj(q0, q1):
                sp.dma_start(adjm[:, q0:q1], adj_v[:, q0:q1]).then_inc(s_adj[q0 > 0], 16)

            load_adj(0, QT // 2)
            load_adj(QT // 2, QT)
            for dst, src in ((bvb[:], bv), (bob[:], bo)):
                sp.dma_start(dst, src.rearrange("(o e) -> o e", o=1).to_broadcast([P, E])).then_inc(s_bcast, 16)
            for n, g in enumerate((g_xattn, g_ffn)):
                sp.dma_start(gr[:, n:n + 1], g.rearrange("(o e) -> o e", o=1).to_broadcast([P, 1])).then_inc(s_bcast, 16)

            def stack_parts(b, par):
                for t in range(2):
                    for m in range(EC):
                        sp.wait_ge(s_parts, b * 4 + (2 * t + m + 1))
                        sp.dma_start(part_d[par, t, :, m * P:(m + 1) * P, :].rearrange("o a p s -> p (o a) s"),
                                     parts[:, t, m]).then_inc(s_partd[t], 16)
                for t in range(2):
                    sp.wait_ge(s_partd[t], b * 32 + 32)
                    for j, part in enumerate((Q_PART, K_PART)[t]):
                        sp.dma_start(stack[D * j:D * (j + 1), par, t].rearrange("p o h s -> p (o h) s"),
                                     part_d[par, t, part].rearrange("o (h d) s -> d (o h) s", d=D)
                                     ).then_inc(s_stack, 16)

            stack_parts(0, ds(0, 1))
            def load_xres(t, u):
                sp.dma_start(xres[:, u], xt_v[ds(t, 1)].rearrange("b p e -> p (b e)")).then_inc(t_x[u], 16)

            def tail_pair(b, t, k, nxt):
                for u in range(2):
                    sp.wait_ge(t_x1, b * 4 + k + u + 1)
                    if nxt is not None:
                        load_xres(nxt + u, u)
                for u in range(2):
                    sp.wait_ge(t_row, b * 4 + k + u + 1)
                    sp.dma_start(rows_d[ds((t + u) * P, P), :], rows[:, u]).then_inc(t_out[u], 16)
                for u in range(2):
                    sp.wait_ge(t_out[u], b * 32 + (8 * k + 16))
                    sp.wait_ge(t_x2T, b * 4 + k + u + 1)
                    sp.sem_inc(t_rowfree, 1)

            for u in range(2):
                load_xres(NT - 2 + u, u)
            with sp.Fori(0, B - 1) as b:
                sp.wait_ge(s_p0, b * 4 + 4)
                sp.dma_start(xin[:], x_v[ds(b + 1, 1)].rearrange("b p t e -> p (b t) e")).then_inc(s_x, 16)
                sp.dma_start(cin[:], c_v[ds(b + 1, 1)].rearrange("b p t e -> p (b t) e")).then_inc(s_ctx, 16)
                sp.wait_ge(s_adjm, b * QT + QT)
                sp.dma_start(maski[:], m_v[ds(b + 1, 1)].rearrange("b p t e -> p (b t) e")).then_inc(s_mask, 16)
                tail_pair(b, (b * QT + (NT - 2)) % NT, 0, b * QT)
                sp.wait_ge(s_masked, b * TILES + TILES // 2)
                load_adj(0, QT // 2)
                stack_parts(b + 1, ds((b + 1) % 2, 1))
                tail_pair(b, b * QT, 2, b * QT + 2)
                sp.wait_ge(s_masked, b * TILES + TILES)
                load_adj(QT // 2, QT)

            def load_w2(e):
                sp.dma_start(w2s[:, e], w2[e].rearrange("(c p) f -> p c f", p=P)).then_inc(r_w2, 16)

            last = B - 1
            tail_pair(last, last * QT - 2, 0, last * QT)
            sp.wait_ge(s_score, last * TILES)
            for e in range(X // 2):
                load_w2(e)
            tail_pair(last, last * QT, 2, last * QT + 2)
            sp.wait_ge(s_adjm, B * QT)
            sp.dma_start(b2b, b2.rearrange("(o x) e -> o (x e)", o=1).to_broadcast([P, X * E]).rearrange(
                "p (x e) -> p x e", x=X)).then_inc(r_b2, 16)
            sp.wait_ge(s_score, B * TILES)
            for e in range(X // 2, X):
                load_w2(e)
            tail_pair(B, NT - 2, 0, None)
            sp.wait_ge(r_eid, 1)

            def load_slots(s, u):
                at = sp.value_load(base_i[0:1, ds(s, 1)], min_val=0, max_val=X * TOK)
                sp.dma_start(slots[:, ds(s, 1), :].rearrange("p s a -> p (s a)"),
                             slot_d[ds(at, P), :]).then_inc(r_slots[u], 16)

            def load_w1(s, u):
                e = sp.value_load(eid[0:1, ds(s, 1)], min_val=0, max_val=X - 1)
                sp.dma_start(w1s[:, u], w1_v[ds(e, 1)].rearrange("x p k f -> p (x k) f")).then_inc(f_w1[u], 16)

            sp.wait_ge(r_free, B + 2)
            for u in range(2):
                load_slots(u, u)
            for u in range(2):
                load_w1(u, u)
            with sp.Fori(0, (SLOTS - 3) // 2) as i:
                for u in range(2):
                    sp.wait_ge(f_h, i * (2 * FC) + FC * (u + 1))
                    load_slots(i * 2 + (u + 2), u)
                    load_w1(i * 2 + (u + 2), u)
            sp.wait_ge(f_h, FC * (SLOTS - 2))
            load_slots(SLOTS - 1, 0)
            load_w1(SLOTS - 1, 0)
            for u in range(2):
                sp.wait_ge(f_sc[u], 16 * ((SLOTS + 1 - u) // 2))

        @block.gpsimd
        def _(po):
            po.memset(ident[:], 0.0).then_inc(s_const, 1)
            po.memset(ones[:], 1.0).then_inc(s_const, 1)
            po.memset(minus_half[:], -0.5).then_inc(s_half, 1)
            po.memset(vals[:], 0.0).then_inc(s_vinit, 1)
            po.wait_ge(s_const, 2)
            po.affine_select(out=ident[:], in_=ident[:], compare_op=ALU.not_equal, fill=1.0, base=0,
                             pattern=[[-1, P]], channel_multiplier=1).then_inc(s_const, 1)
            po.wait_ge(s_vinit, 1)
            po.memset(vals[:, :, :, D:D + 1], 1.0).then_inc(s_vinit, 1)
            po.affine_select(out=ltri[:], in_=ones[:], compare_op=ALU.is_gt, fill=0.0, base=0,
                             pattern=[[1, P]], channel_multiplier=-1).then_inc(s_const, 1)
            po.iota(ids[:].rearrange("p b t -> p (b t)"), pattern=[[P, (B + 1) * QT]], base=-S,
                    channel_multiplier=1).then_inc(s_const, 1)
            n = 5

            def numbers(dst, width, step, base):
                nonlocal n
                po.wait_ge(s_const, n)
                po.iota(iot[:, 0:width], pattern=[[step, width]], base=base,
                        channel_multiplier=0).then_inc(s_const, 1)
                po.wait_ge(s_const, n + 1)
                po.tensor_copy(dst, iot[:, 0:width]).then_inc(s_const, 1)
                n += 2

            numbers(seven[:], X, -1, X)
            numbers(region[:], X, TOK, 0)
            numbers(region0[:], X, TOK, 0)
            numbers(thr[:], NT, P, 0)
            numbers(slotn[:], SLOTS_R, 1, 0)
            po.memset(live[:, 0:1], 0.0).then_inc(s_const, 1)
            po.memset(live[:, 1:], 1.0).then_inc(s_const, 1)
            po.memset(dead[:, 0:1], 1e6).then_inc(s_const, 1)
            po.memset(dead[:, 1:], 0.0).then_inc(s_const, 1)
            po.memset(o_sb[:, :, 1, :], 1.0).then_inc(t_ones, 1)
            po.memset(logit[:], 0.0).then_inc(t_ones, 1)
            po.memset(empty[:, :, 0], TOK).then_inc(r_init, 1)
            po.memset(empty[:, :, 1], 0).then_inc(r_init, 1)
            po.memset(zrow, 0.0).then_inc(r_init, 1)
            po.wait_ge(r_init, 3)
            po.dma_start(slot_d[0:X * TOK].rearrange("(p s) a -> p s a", p=P), empty[:]).then_inc(r_fill, 16)
            po.dma_start(slot_d[X * TOK:], empty[:, 0]).then_inc(r_fill, 16)
            po.dma_start(rows_d[TOK:TOK + 1, :], zrow).then_inc(r_fill, 16)

            def masks(b, q0, q1):
                wait_apart(po, s_adj[q0 > 0], b * 16 + 16)
                for qt in range(q0, q1):
                    mf = maski[:, qt].bitcast(F32)
                    po.tensor_scalar(mf, maski[:, qt], 0.0, SHUT, ALU.is_equal, ALU.mult).then_inc(s_penal, 1)
                    po.wait_ge(s_penal, b * QT + qt + 1)
                    po.tensor_tensor(adjm[:, qt], mf, adjm[:, qt], ALU.add).then_inc(s_adjm, 1)

            def norm(b):
                wait_apart(po, s_mv, b * QT + QT)
                po.tensor_scalar(mv[:, :, 1], mv[:, :, 1], EPS, None, ALU.add).then_inc(s_eps, 1)
                po.wait_ge(s_eps, b + 1)
                po.tensor_tensor(rstd[:], mv[:, :, 1], minus_half[:], ALU.pow).then_inc(s_rstd, 1)

            po.wait_ge(s_half, 1)
            norm(0)
            po.wait_ge(s_mask, 16)
            masks(0, 0, QT // 2)
            masks(0, QT // 2, QT)

            def tail_rstd(b, k):
                for u in range(2):
                    wait_apart(po, t_mv, b * 4 + k + u + 1)
                    po.tensor_scalar(mv2[:, u, 1:2], mv2[:, u, 1:2], EPS, None, ALU.add).then_inc(t_eps, 1)
                    po.wait_ge(t_eps, b * 4 + k + u + 1)
                    po.tensor_tensor(rstd2[:, u:u + 1], mv2[:, u, 1:2], minus_half[:, 0:1],
                                     ALU.pow).then_inc(t_rstd, 1)

            def to_slots(b):
                po.tensor_copy(pair[:, :, 0], ids[:, ds(b, 1), :].rearrange("p b t -> p (b t)")).then_inc(r_ids, 1)
                po.wait_ge(r_ids, b + 1)
                po.wait_ge(r_wt, b + 1)
                wait_apart(po, r_pair, b + 1)
                for t in range(QT):
                    po.indirect_dma_start(slot_d, bass.IndirectOffsetOnAxis(ap=posi[:, t:t + 1], axis=0),
                                          pair[:, t], None, bounds_check=X * TOK - 1,
                                          oob_is_err=False).then_inc(r_scat, 16)
                po.wait_ge(r_scat, b * (16 * QT) + 16 * QT)
                po.sem_inc(r_free, 1)

            po.wait_ge(r_fill, 48)
            with po.Fori(0, B - 1) as b:
                tail_rstd(b, 0)
                norm(b + 1)
                to_slots(b)
                wait_apart(po, s_mask, b * 16 + 32)
                masks(b + 1, 0, QT // 2)
                tail_rstd(b, 2)
                masks(b + 1, QT // 2, QT)
            tail_rstd(B - 1, 0)
            to_slots(B - 1)
            tail_rstd(B - 1, 2)
            tail_rstd(B, 0)
            to_slots(B)

            def gather(s, i, u):
                po.wait_ge(r_slots[u], i * 16 + 16)
                po.tensor_copy(gidx[:, u:u + 1], slots[:, ds(s, 1), 0]).then_inc(f_gi, 1)
                wait_apart(po, f_gi, s + 1)
                po.indirect_dma_start(rows[:, u], None, rows_d,
                                      bass.IndirectOffsetOnAxis(ap=gidx[:, u:u + 1], axis=0)
                                      ).then_inc(f_row[u], 16)

            def scatter(s, u):
                po.tensor_copy(sidx[:, u:u + 1], slots[:, ds(s, 1), 0]).then_inc(f_si, 1)
                wait_apart(po, f_si, s + 1)
                po.indirect_dma_start(out_v, bass.IndirectOffsetOnAxis(ap=sidx[:, u:u + 1], axis=0),
                                      orow[:, u], None, bounds_check=TOK - 1,
                                      oob_is_err=False).then_inc(f_sc[u], 16)

            def scattered(i, u):
                po.wait_ge(f_sc[u], i * 16 + 16)
                po.sem_inc(f_free, 1)

            for u in range(2):
                gather(u, 0, u)
            with po.Fori(0, (SLOTS - 3) // 2) as i:
                for u in range(2):
                    po.wait_ge(f_out, i * 2 + u + 1)
                    gather(i * 2 + (u + 2), i + 1, u)
                    scatter(i * 2 + u, u)
                    scattered(i, u)
            for s in range(SLOTS - 3, SLOTS):
                po.wait_ge(f_out, s + 1)
                if s + 2 < SLOTS:
                    gather(s + 2, s // 2 + 1, s % 2)
                scatter(s, s % 2)
                scattered(s // 2, s % 2)

        @block.tensor
        def _(pe):
            def bank_free(b, i):
                k = SETUP + NEXT + i
                if not isinstance(b, int) or b > 0 or k >= 2:
                    pe.wait_ge(s_md[k % 2], free(b, i))
                return sp_bank[k % 2]

            pe.wait_ge(s_const, 3)
            pe.wait_ge(s_wraw, 64)
            for w in range(4):
                bank_free(0, w - SETUP - NEXT)
                for k in range(EC):
                    for m in range(EC):
                        mm = pe.transpose(sp_bank[w % 2][:, k * E + m * P:k * E + (m + 1) * P],
                                          wraw[:, w, m, k * P:(k + 1) * P], ident[:])
                mm.then_inc(s_m, 1)
            pe.wait_ge(s_small, 64)
            bank_free(0, 4 - SETUP - NEXT)
            nr = X * FC + 2 * EC
            pe.transpose(sp_bank[0][:, 0:nr], rowsm, ident[0:nr, 0:nr]).then_inc(s_m, 1)
            bank_free(0, 5 - SETUP - NEXT)
            for k in range(EC):
                mm = pe.transpose(sp_bank[1][:, k * X:(k + 1) * X], gate_r[:, k * P:(k + 1) * P],
                                  ident[0:X, 0:X])
            mm.then_inc(s_m, 1)

            def turn_in(b, i, src, k):
                o = bank_free(b, i)
                for t in range(QT):
                    mm = pe.transpose(o[:, t * P:(t + 1) * P], src[:, t, k * P:(k + 1) * P], ident[:])
                mm.then_inc(s_m, 1)

            def project(b, i, w, src, m):
                o = bank_free(b, i)
                for k in range(EC):
                    mm = pe.matmul(o[:], wT[:, w, k, m * P:(m + 1) * P], src[:, k],
                                   start=k == 0, stop=k == EC - 1)
                mm.then_inc(s_m, 1)

            def next_use(b, i, what, k, nxt):
                if what == "next x":
                    if k == 0:
                        pe.wait_ge(s_xn, nxt * QT + QT)
                    turn_in(b, i, xin, k)
                if what == "next ctx":
                    if k == 0:
                        pe.wait_ge(s_ctx, nxt * 16 + 16)
                    turn_in(b, i, cin, k)
                if what == "next q":
                    if k == 0:
                        pe.wait_ge(s_xT, nxt * 4 + 2)
                    project(b, i, 0, xT, k)
                if what == "next k":
                    if k == 0:
                        pe.wait_ge(s_xT, nxt * 4 + 4)
                    project(b, i, 1, cT, k)

            def values(b, i, h):
                o = bank_free(b, i)
                for t in range(2):
                    for k in range(EC):
                        mm = pe.matmul(o[:, t * E:(t + 1) * E], cT[:, k, (2 * h + t) * P:(2 * h + t + 1) * P],
                                       wT[:, 2, k], start=k == 0, stop=k == EC - 1)
                mm.then_inc(s_m, 1)

            def tail_use(b, i, what, k):
                if what == "rank":
                    pe.wait_ge(r_oh, b + 1)
                    o = bank_free(b, i)
                    for t in range(QT):
                        pe.matmul(o[:, QT * X:(QT + 1) * X], ones[:], onehot[:, t], start=t == 0,
                                  stop=t == QT - 1)
                    pe.matmul(o[:, 0:QT * X], ltri[:], onehot[:].rearrange("p t x -> p (t x)"), start=True,
                              stop=False)
                    for t in range(QT - 1):
                        for t2 in range(t + 1, QT):
                            mm = pe.matmul(o[:, t2 * X:(t2 + 1) * X], ones[:], onehot[:, t], start=False,
                                           stop=t == QT - 2)
                    mm.then_inc(s_m, 1)
                    return
                if what == "gate":
                    pe.wait_ge(t_x2T, b * 4 + k[-1] + 1)
                    o = bank_free(b, i)
                    for j, kk in enumerate(k):
                        for c in range(EC):
                            mm = pe.matmul(o[:, j * X:(j + 1) * X], x2T[:, kk % 2, c], gateT[:, c],
                                           start=c == 0, stop=c == EC - 1)
                    mm.then_inc(s_m, 1)
                    return
                u = k % 2
                if what == "heads":
                    o = bank_free(b, i)
                    for a in range(NG):
                        mm = pe.transpose(o[:, a * P:(a + 1) * P], o_sb[:, a, int(k < 2), u * P:(u + 1) * P],
                                          ident[:])
                if what == "turn":
                    pe.wait_ge(t_attn, b * 4 + k + 1)
                    o = bank_free(b, i)
                    for c in range(EC):
                        mm = pe.transpose(o[:, c * P:(c + 1) * P], attn[:, u, c * P:(c + 1) * P], ident[:])
                if what == "out":
                    pe.wait_ge(t_atT, b * 4 + k + 1)
                    o = bank_free(b, i)
                    for c in range(EC):
                        mm = pe.matmul(o[:, 0:E], atT[:, u, c], wT[:, 3, c], start=c == 0, stop=c == EC - 1)
                if what == "normed":
                    pe.wait_ge(t_row, b * 4 + k + 1)
                    o = bank_free(b, i)
                    for c in range(EC):
                        mm = pe.transpose(o[:, c * P:(c + 1) * P], rows[:, u, E + c * P:E + (c + 1) * P],
                                          ident[:])
                mm.then_inc(s_m, 1)

            def scores(b, par, n):
                g, qt, q2, h, j = tile_of(n)
                if n >= NS:
                    pe.wait_ge(s_masked, b * TILES + (n - NS + 1))
                q = stack[:, par, 0, h, qt * P:(qt + 1) * P].rearrange("p o q -> p (o q)")
                k = stack[:, par, 1, h, :].rearrange("p o q -> p (o q)")
                pe.matmul(sc_bank[n % NS][:], q, k, start=True, stop=True).then_inc(s_score, 1)

            def transposes(b, n):
                pe.wait_ge(s_exp, b * TILES + n + 1)
                if n >= NTB:
                    if (n - NTB) % 8 in DVE_COPIES:
                        pe.wait_ge(s_cdve, b * dve_copies(TILES) + dve_copies(n - NTB + 1))
                    else:
                        pe.wait_ge(s_cact, b * act_copies(TILES) + act_copies(n - NTB + 1))
                for c in range(QT):
                    mm = pe.transpose(tr_bank[n % NTB][:, c * P:(c + 1) * P], prob[:, n % NB, c * P:(c + 1) * P],
                                      ident[:])
                mm.then_inc(s_trans, 1)

            def weigh(b, g):
                pe.wait_ge(s_cact, b * act_copies(TILES) + act_copies(TPG * (g + 1)))
                pe.wait_ge(s_cdve, b * dve_copies(TILES) + dve_copies(TPG * (g + 1)))
                if g >= 2:
                    pe.wait_ge(s_osb, b * GROUPS + (g - 1))
                hg = g % NG
                for c in range(QT):
                    for j in range(HG):
                        mm = pe.matmul(pv_bank[32 * j:32 * j + 32, (g % 2) * HALF:(g % 2 + 1) * HALF],
                                       vals[:, c, hg * HG + j, :], pt[:, g % 2, c, j, :],
                                       start=c == 0, stop=c == QT - 1)
                mm.then_inc(s_pv, 1)

            def attention(b, par, uses):
                pe.wait_ge(s_stack, b * (32 * PAIRS) + 32 * PAIRS)
                for n in range(TILES + LP + 1):
                    if n < TILES:
                        scores(b, par, n)
                    if LT <= n < TILES + LT:
                        transposes(b, n - LT)
                    if n >= LP + TPG and (n - LP) % TPG == 0:
                        if n == LP + TPG:
                            pe.wait_ge(s_v, b * 2 + 2)
                        weigh(b, (n - LP) // TPG - 1)
                    for i, what, k in at_step(uses, n):
                        if n == 39 and k == 2:
                            pe.wait_ge(s_osb, b * GROUPS + NG)
                        if what == "values":
                            values(b, i, k)
                        elif what.startswith("next"):
                            next_use(b, i, what, k, b + 1)
                        else:
                            tail_use(b, i, what, k)
                pe.wait_ge(s_osb, b * GROUPS + GROUPS)

            for j, (n, what, k) in enumerate(NEXT_USES):
                next_use(0, j - NEXT, what, k, 0)
            pe.wait_ge(t_ones, 2)
            with pe.Fori(0, B - 1) as b:
                attention(b, ds(b % 2, 1), USES)
            attention(B - 1, ds((B - 1) % 2, 1), LAST_USES)
            for i, (n, what, k) in enumerate(TAIL_A):
                tail_use(B, i + LAST_SHIFT, what, k)

            def expert(s, i, u):
                e = pe.value_load(eid[0:1, ds(s, 1)], min_val=0, max_val=X - 1)
                pe.wait_ge(f_row[u], i * 16 + 16)
                for k in range(EC):
                    mm = pe.transpose(bank[4 * u][:, k * P:(k + 1) * P], rows[:, u, E + k * P:E + (k + 1) * P],
                                      ident[:])
                mm.then_inc(f_xt, 1)
                pe.wait_ge(f_w1[u], i * 16 + 16)
                pe.wait_ge(f_xgT, s + 1)
                for c in range(FC):
                    o = bank[4 * u + 1 + c // 4][:, (c % 4) * P:(c % 4 + 1) * P]
                    for k in range(EC):
                        mm = pe.matmul(o, w1s[:, u, k, c * P:(c + 1) * P], xgT[:, u, k],
                                       start=k == 0, stop=k == EC - 1)
                    mm.then_inc(f_h, 1)
                for c in range(FC):
                    pe.wait_ge(f_hT, s * FC + c + 1)
                    mm = pe.matmul(bank[4 * u + 3][:, 0:E], hT[:, u, c],
                                   w2s[:, ds(e, 1), c, :].rearrange("p x e -> p (x e)"),
                                   start=c == 0, stop=c == FC - 1)
                mm.then_inc(f_y, 1)

            pe.wait_ge(r_eid, 1)
            pe.wait_ge(r_w2, 16 * X)
            with pe.Fori(0, SLOTS // 2) as i:
                for u in range(2):
                    expert(i * 2 + u, i, u)
            expert(SLOTS - 1, SLOTS // 2, 0)

        @block.scalar
        def _(act):
            for w in range(4):
                act.wait_ge(s_m, w + 1)
                act.activation(wT[:, w], sp_bank[w % 2][:].rearrange("p (k f) -> p k f", k=EC), ACT.Copy,
                               scale=float(D) ** -0.5 if w == 0 else 1.0).then_inc(s_md[w % 2], 1)
            act.wait_ge(s_m, 5)
            act.activation(colsm[:], sp_bank[0][:, 0:X * FC + 2 * EC], ACT.Copy).then_inc(s_tg, 1)
            act.wait_ge(s_tg, 1)
            act.activation(bqc, bqc, ACT.Copy, scale=float(D) ** -0.5).then_inc(s_md[0], 1)
            act.wait_ge(s_m, 6)
            act.activation(gateT[:].rearrange("p k x -> p (k x)"), sp_bank[1][:, 0:EC * X],
                           ACT.Copy).then_inc(s_md[1], 1)
            act.wait_ge(s_bcast, 64)
            act.activation(tg[:], gr[:], ACT.Tanh).then_inc(s_tg, 1)
            act.wait_ge(s_md[0], 3)

            def next_use(b, i, what, k, nxt):
                o = sp_bank[i % 2]
                act.wait_ge(s_m, ready(b, i))
                if what in ("next x", "next ctx"):
                    dst = xT if what == "next x" else cT
                    act.activation(dst[:, k], o[:], ACT.Copy).then_inc(s_xT, 1)
                    act.wait_ge(s_xT, nxt * 4 + (1 if what == "next x" else 3) + k)
                    act.sem_inc(s_md[i % 2], 1)
                else:
                    t = int(what == "next k")
                    if not (isinstance(nxt, int) and nxt == 0):
                        act.wait_ge(s_partd[t], nxt * 32)
                    act.activation(parts[:, t, k, 0], o[:], ACT.Identity,
                                   bias=(bqc, bkc)[t][:, k:k + 1]).then_inc(s_p0, 1)

            def tail_use(b, i, what, k):
                if what not in ("turn", "normed"):
                    return
                act.wait_ge(s_m, ready(b, i))
                dst, done = (atT, t_atT) if what == "turn" else (x2T, t_x2T)
                act.activation(dst[:, k % 2], sp_bank[i % 2][:, 0:E].rearrange("p (k q) -> p k q", k=EC),
                               ACT.Copy).then_inc(done, 1)
                act.wait_ge(done, b * 4 + k + 1)
                act.sem_inc(s_md[i % 2], 1)

            def route_exp(b):
                act.wait_ge(r_sub, b + 1)
                act.activation(logit[:], logit[:], ACT.Exp).then_inc(r_exp, 1)

            def attention(b, uses):
                for n in range(TILES + LP + 1):
                    c = n - LE
                    if 0 <= c < TILES and c % 8 not in DVE_COPIES:
                        g, qt, q2, h, j = tile_of(c)
                        act.wait_ge(s_trans, b * TILES + c + 1)
                        if g >= 2:
                            act.wait_ge(s_pv, b * GROUPS + (g - 1))
                        act.activation(pt[:, g % 2, :, j, q2 * P:(q2 + 1) * P],
                                       tr_bank[c % NTB][:].rearrange("p (c q) -> p c q", c=QT),
                                       ACT.Copy).then_inc(s_cact, 1)
                    if n < TILES:
                        act.wait_ge(s_masked, b * TILES + n + 1)
                        act.activation(prob[:, n % NB], prob[:, n % NB], ACT.Exp, scale=-1.0,
                                       bias=negmax[:, n % NB:n % NB + 1]).then_inc(s_exp, 1)
                    for i, what, k in at_step(uses, n - 1):
                        if what.startswith("next"):
                            next_use(b, i, what, k, b + 1)
                        else:
                            tail_use(b, i, what, k)
                    if n == 20:
                        route_exp(b)
                act.wait_ge(s_pv, b * GROUPS + GROUPS)

            for j, (n, what, k) in enumerate(NEXT_USES):
                next_use(0, j - NEXT, what, k, 0)
            with act.Fori(0, B - 1) as b:
                attention(b, USES)
            attention(B - 1, LAST_USES)
            for i, (n, what, k) in enumerate(TAIL_A):
                tail_use(B, i + LAST_SHIFT, what, k)
            route_exp(B)

            def expert(s, i, u):
                e = act.value_load(eid[0:1, ds(s, 1)], min_val=0, max_val=X - 1)
                act.wait_ge(f_xt, s + 1)
                act.activation(xgT[:, u], bank[4 * u][:, 0:E].rearrange("p (k q) -> p k q", k=EC),
                               ACT.Copy).then_inc(f_xgT, 1)
                for c in range(FC):
                    if c % 4 == 0:
                        act.wait_ge(f_h, s * FC + c + 4)
                    act.activation(hT[:, u, c], bank[4 * u + 1 + c // 4][:, (c % 4) * P:(c % 4 + 1) * P],
                                   ACT.Relu, bias=b1c[:, ds(e * FC + c, 1)]).then_inc(f_hT, 1)

            act.wait_ge(r_eid, 1)
            with act.Fori(0, SLOTS // 2) as i:
                for u in range(2):
                    expert(i * 2 + u, i, u)
            expert(SLOTS - 1, SLOTS // 2, 0)

        @block.vector
        def _(ve):
            ve.wait_ge(s_tg, 2)

            def norm_stats(b):
                ve.wait_ge(s_x, b * 16 + 16)
                for t in range(QT):
                    ve.bn_stats(stats[:, t], xin[:, t]).then_inc(s_stat, 1)
                for t in range(QT):
                    wait_apart(ve, s_stat, b * QT + t + 1)
                    ve.bn_aggr(mv[:, t], stats[:, t]).then_inc(s_mv, 1)

            def norm(b):
                ve.wait_ge(s_rstd, b + 1)
                for t in range(QT):
                    ve.tensor_scalar(xin[:, t], xin[:, t], mv[:, t, 0:1], rstd[:, t:t + 1],
                                     ALU.subtract, ALU.mult).then_inc(s_xn, 1)

            def next_use(b, i, what, m, nxt):
                if what not in ("next q", "next k"):
                    return
                t = int(what == "next k")
                k = 2 * t + m + 1
                ve.wait_ge(s_p0, nxt * 4 + k)
                if not isinstance(nxt, int) or k > 1:
                    ve.wait_ge(s_parts, nxt * 4 + (k - 1))
                ve.scalar_tensor_tensor(out=rest[:], in0=sp_bank[i % 2][:], scalar=(bqc, bkc)[t][:, m:m + 1],
                                        in1=parts[:, t, m, 0], op0=ALU.add, op1=ALU.subtract
                                        ).then_inc(s_md[i % 2], 1)
                ve.wait_ge(s_md[i % 2], free(b, i) + 1)
                ve.tensor_copy(parts[:, t, m, 1], rest[:]).then_inc(s_p1, 1)
                ve.wait_ge(s_p1, nxt * 4 + k)
                ve.tensor_tensor(parts[:, t, m, 2], rest[:], parts[:, t, m, 1], ALU.subtract).then_inc(s_parts, 1)

            def values(b, i, h):
                ve.wait_ge(s_m, ready(b, i))
                for t in range(2):
                    ins = ve.tensor_tensor(vals[:, 2 * h + t, :, 0:D],
                                           sp_bank[i % 2][:, t * E:(t + 1) * E].rearrange("p (h d) -> p h d", d=D),
                                           bvb[:].rearrange("p (h d) -> p h d", d=D), ALU.add)
                    ins.then_inc((s_rest, s_v)[t], 1)
                ve.wait_ge(s_v, b * 2 + h + 1)
                ve.wait_ge(s_rest, b * 2 + h + 1)
                ve.sem_inc(s_md[i % 2], 1)

            def tail_use(b, i, what, k):
                o = sp_bank[i % 2]
                if what == "heads":
                    u = k % 2
                    o4 = o[:].rearrange("p (h w) -> p h w", w=VW)
                    ve.wait_ge(s_m, ready(b, i))
                    ve.reciprocal(rinv[:, u], o4[:, :, D]).then_inc(t_rinv, 1)
                    ve.wait_ge(t_rinv, b * 4 + k + 1)
                    ve.tensor_tensor(attn[:, u].rearrange("p (h d) -> p h d", d=D), o4[:, :, 0:D],
                                     rinv[:, u].rearrange("p (h o) -> p h o", o=1).to_broadcast([P, H, D]),
                                     ALU.mult).then_inc(t_attn, 1)
                    ve.wait_ge(t_attn, b * 4 + k + 1)
                    ve.sem_inc(s_md[i % 2], 1)
                if what == "out":
                    u = k % 2
                    r = rows[:, u]
                    ve.wait_ge(s_m, ready(b, i))
                    ve.wait_ge(t_x[u], b * 32 + (8 * (k - u) + 16))
                    ve.wait_ge(t_rowfree, b * 4 + k + 1)
                    ve.tensor_tensor(r[:, 0:E], o[:, 0:E], bob[:], ALU.add).then_inc(s_md[i % 2], 1)
                    ve.wait_ge(s_md[i % 2], free(b, i) + 1)
                    ve.scalar_tensor_tensor(out=r[:, 0:E], in0=r[:, 0:E], scalar=tg[:, 0:1], in1=xres[:, u],
                                            op0=ALU.mult, op1=ALU.add).then_inc(t_x1, 1)
                    ve.wait_ge(t_x1, b * 4 + k + 1)
                    ve.bn_stats(st2[:, u], r[:, 0:E]).then_inc(t_stat, 1)
                    wait_apart(ve, t_stat, b * 4 + k + 1)
                    ve.bn_aggr(mv2[:, u], st2[:, u]).then_inc(t_mv, 1)
                if what == "gate":
                    ve.wait_ge(s_m, ready(b, i))
                    t = (k[0] + 2) % 4
                    ve.tensor_copy(logit[:, t:t + len(k), :].rearrange("p t x -> p (t x)"),
                                   o[:, 0:len(k) * X]).then_inc(s_md[i % 2], 1)
                if what == "rank":
                    ve.wait_ge(s_m, ready(b, i))
                    place_tokens(b, i, o)

            def norm_row(b, k):
                u = k % 2
                r = rows[:, u]
                ve.wait_ge(t_rstd, b * 4 + k + 1)
                ve.tensor_scalar(r[:, E:2 * E], r[:, 0:E], mv2[:, u, 0:1], rstd2[:, u:u + 1],
                                 ALU.subtract, ALU.mult).then_inc(t_row, 1)

            def per_tile(ap):
                return ap.rearrange("p (t o) -> p t o", o=1).to_broadcast([P, QT, X])

            def per_expert(ap):
                return ap.rearrange("p (o x) -> p o x", o=1).to_broadcast([P, QT, X])

            ROUTE_LINKS = 9

            class Links:
                k = 0

            def link(ins, b):
                Links.k += 1
                ins.then_inc(r_dve, 1)
                ve.wait_ge(r_dve, b * ROUTE_LINKS + Links.k)

            def route_shift(b, i):
                ve.wait_ge(s_md[i % 2], free(b, i) + 1)
                Links.k = 0
                link(ve.tensor_reduce(mx[:], logit[:], AX.X, ALU.max), b)
                ve.tensor_tensor(logit[:], logit[:], per_tile(mx[:]), ALU.subtract).then_inc(r_sub, 1)

            def route_pick(b):
                ve.wait_ge(r_free, b + 1)
                ve.wait_ge(r_exp, b + 1)
                link(ve.tensor_reduce(sm[:], logit[:], AX.X, ALU.add), b)
                link(ve.tensor_reduce(em[:], logit[:], AX.X, ALU.max), b)
                link(ve.tensor_tensor(key[:], logit[:], per_tile(em[:]), ALU.is_equal), b)
                link(ve.tensor_tensor(key[:], key[:], per_expert(seven[:]), ALU.mult), b)
                link(ve.tensor_reduce(km[:], key[:], AX.X, ALU.max), b)
                ve.scalar_tensor_tensor(out=onehot[:], in0=key[:], scalar=live[:, ds(b, 1)], in1=per_tile(km[:]),
                                        op0=ALU.mult, op1=ALU.is_equal).then_inc(r_oh, 1)
                link(ve.reciprocal(wt[:], sm[:]), b)
                link(ve.tensor_tensor(wt[:], wt[:], em[:], ALU.mult), b)
                ve.tensor_scalar(pair[:].bitcast(F32)[:, :, 1], wt[:], tg[:, 1:2], None, ALU.mult).then_inc(r_wt, 1)

            def place_tokens(b, i, o):
                ve.tensor_tensor(place[:], o[:, 0:QT * X].rearrange("p (t x) -> p t x", x=X),
                                 per_expert(region[:]), ALU.add).then_inc(r_mx, 1)
                ve.wait_ge(r_mx, b + 1)
                ve.tensor_tensor(region[:], region[:], o[:, QT * X:(QT + 1) * X], ALU.add).then_inc(s_md[i % 2], 1)
                ve.tensor_tensor(place[:], place[:], onehot[:], ALU.mult).then_inc(r_st, 1)
                ve.wait_ge(r_st, b + 1)
                link(ve.tensor_reduce(posf[:], place[:], AX.X, ALU.add), b)
                assert Links.k == ROUTE_LINKS
                ve.tensor_scalar(posi[:], posf[:], dead[:, ds(b, 1)], None, ALU.add).then_inc(r_pair, 1)

            def attention(b, uses):
                gate_i = next(i for i, (n, w, k) in enumerate(uses) if w == "gate")
                for n in range(TILES + LP + 1):
                    c = n - LE
                    if 0 <= c < TILES and c % 8 in DVE_COPIES:
                        g, qt, q2, h, j = tile_of(c)
                        ve.wait_ge(s_trans, b * TILES + c + 1)
                        if g >= 2:
                            ve.wait_ge(s_pv, b * GROUPS + (g - 1))
                        ve.tensor_copy(pt[:, g % 2, :, j, q2 * P:(q2 + 1) * P],
                                       tr_bank[c % NTB][:].rearrange("p (c q) -> p c q", c=QT)).then_inc(s_cdve, 1)
                    if n < TILES:
                        g, qt, q2, h, j = tile_of(n)
                        if n % (TILES // 2) == 0:
                            ve.wait_ge(s_adjm, b * QT + (qt + QT // 2))
                        if n >= NB:
                            ve.wait_ge(s_trans, b * TILES + (n - NB + 1))
                        wait_apart(ve, s_score, b * TILES + n + 1)
                        ve.tensor_tensor_reduce(out=prob[:, n % NB], in0=sc_bank[n % NS][:], in1=adjm[:, qt],
                                                scale=-1.0, scalar=BIG, op0=ALU.add, op1=ALU.min,
                                                accum_out=negmax[:, n % NB:n % NB + 1]).then_inc(s_masked, 1)
                    if n >= LP + TPG and (n - LP) % TPG == 0:
                        g = (n - LP) // TPG - 1
                        ve.wait_ge(s_pv, b * GROUPS + g + 1)
                        ve.tensor_copy(o_sb[:, g % NG, g // NG], pv_bank[:, (g % 2) * HALF:(g % 2 + 1) * HALF]
                                       ).then_inc(s_osb, 1)
                    for i, what, k in at_step(uses, n - 1):
                        if what == "values":
                            values(b, i, k)
                        elif what.startswith("next"):
                            next_use(b, i, what, k, b + 1)
                        else:
                            tail_use(b, i, what, k)
                    if n in ROW_STEPS:
                        norm_row(b, ROW_STEPS[n])
                    if n == 18:
                        route_shift(b, gate_i)
                    if n == 21:
                        route_pick(b)
                    if uses is USES:
                        if n == 11:
                            norm_stats(b + 1)
                        if n == 19:
                            norm(b + 1)
                ve.wait_ge(s_trans, b * TILES + TILES)

            norm_stats(0)
            norm(0)
            for j, (n, what, k) in enumerate(NEXT_USES):
                next_use(0, j - NEXT, what, k, 0)
            ve.wait_ge(s_bcast, 64)
            ve.wait_ge(s_vinit, 2)
            ve.wait_ge(s_const, 19)
            ve.wait_ge(t_ones, 2)
            ve.wait_ge(r_fill, 48)
            ve.sem_inc(t_rowfree, 2)
            ve.sem_inc(r_free, 1)
            with ve.Fori(0, B - 1) as b:
                attention(b, USES)
            attention(B - 1, LAST_USES)
            for i, (n, what, k) in enumerate(TAIL_A):
                if what == "normed":
                    norm_row(B, k)
                if what == "rank":
                    route_shift(B, i - 1 + LAST_SHIFT)
                    route_pick(B)
                tail_use(B, i + LAST_SHIFT, what, k)

            done = (B + 1) * ROUTE_LINKS

            def then(ins):
                nonlocal done
                done += 1
                ins.then_inc(r_dve, 1)
                ve.wait_ge(r_dve, done)

            last_rank = len(TAIL_A) - 1 + LAST_SHIFT
            ve.wait_ge(s_md[last_rank % 2], free(B, last_rank) + 1)
            then(ve.tensor_tensor(cnt[:], region[:], region0[:], ALU.subtract))
            then(ve.tensor_tensor(cmp_t[:], cnt[:].rearrange("p (x o) -> p x o", o=1).to_broadcast([P, X, NT]),
                                  thr[:].rearrange("p (o t) -> p o t", o=1).to_broadcast([P, X, NT]), ALU.is_gt))
            then(ve.tensor_reduce(tiles[:], cmp_t[:], AX.X, ALU.add))
            then(ve.tensor_scalar(span[:], tiles[:], -float(P), float(TOK), ALU.mult, ALU.add))
            src, dst = tiles, end
            step = 1
            while step < X:
                then(ve.tensor_copy(dst[:, 0:step], src[:, 0:step]))
                then(ve.tensor_tensor(dst[:, step:], src[:, step:], src[:, 0:X - step], ALU.add))
                src, dst = dst, end2 if dst is end else end
                step *= 2
            then(ve.tensor_tensor(cmp_s[:], slotn[:].rearrange("p (s o) -> p s o", o=1).to_broadcast([P, SLOTS_R, X]),
                                  src[:].rearrange("p (o x) -> p o x", o=1).to_broadcast([P, SLOTS_R, X]), ALU.is_ge))
            then(ve.tensor_reduce(ef[:], cmp_s[:], AX.X, ALU.add))
            then(ve.tensor_scalar(eid[:], ef[:], float(X - 1), None, ALU.min))
            then(ve.tensor_tensor(cmp_s[:], cmp_s[:],
                                  span[:].rearrange("p (o x) -> p o x", o=1).to_broadcast([P, SLOTS_R, X]), ALU.mult))
            then(ve.tensor_reduce(bf[:], cmp_s[:], AX.X, ALU.add))
            then(ve.scalar_tensor_tensor(out=bf[:], in0=slotn[:], scalar=float(P), in1=bf[:], op0=ALU.mult,
                                         op1=ALU.add))
            ve.tensor_scalar(base_i[:], bf[:], float(X * TOK), None, ALU.min).then_inc(r_eid, 1)

            def expert(s, i, u):
                e = ve.value_load(eid[0:1, ds(s, 1)], min_val=0, max_val=X - 1)
                ve.wait_ge(f_y, s + 1)
                ve.wait_ge(r_slots[u], i * 16 + 16)
                ve.tensor_tensor(ytmp[:, u], bank[4 * u + 3][:, 0:E],
                                 b2b[:, ds(e, 1), :].rearrange("p x e -> p (x e)"), ALU.add).then_inc(f_tmp, 1)
                ve.wait_ge(f_tmp, s + 1)
                ve.wait_ge(f_free, s + 1)
                ve.scalar_tensor_tensor(out=orow[:, u], in0=ytmp[:, u],
                                        scalar=slots[:].bitcast(F32)[:, ds(s, 1), 1], in1=rows[:, u, 0:E],
                                        op0=ALU.mult, op1=ALU.add).then_inc(f_out, 1)

            ve.sem_inc(f_free, 2)
            ve.wait_ge(r_eid, 1)
            ve.wait_ge(r_b2, 16)
            with ve.Fori(0, SLOTS // 2) as i:
                for u in range(2):
                    expert(i * 2 + u, i, u)
            expert(SLOTS - 1, SLOTS // 2, 0)


_INS = ["x", "ctx_1024", "mask_Bx1xSxS2_ik1", "g_xattn", "g_ffn", "L0_xattn_adj", "L0_xattn_Wq",
        "L0_xattn_bq", "L0_xattn_Wk", "L0_xattn_bk", "L0_xattn_Wv", "L0_xattn_bv", "L0_xattn_Wo",
        "L0_xattn_bo", "L0_ffn_gate_w", "L0_ffn_w1", "L0_ffn_b1", "L0_ffn_w2", "L0_ffn_b2"]


def kernel(**inputs):
    import numpy as np
    import concourse.bacc as bacc
    from concourse.bass_utils import run_bass_kernel_spmd

    nc = bacc.Bacc("TRN2", target_bir_lowering=False, num_devices=1)
    arrays, args = {}, []
    for name in _INS:
        a = np.ascontiguousarray(inputs[name])
        arrays[f"in_{name}"] = a
        args.append(nc.dram_tensor(f"in_{name}", a.shape, mybir.dt.from_np(a.dtype), kind="ExternalInput").ap())
    shape = inputs["x"].shape
    out = nc.dram_tensor("out_y", shape, F32, kind="ExternalOutput").ap()
    build(nc, *args, out)
    r = run_bass_kernel_spmd(nc, [arrays], core_ids=[0])
    return r.results[0]["out_y"]
```

```python
from contextlib import ExitStack

import concourse.bass as bass
from concourse import mybir

ALU = mybir.AluOpType
ACT = mybir.ActivationFunctionType
AX = mybir.AxisListType
F32 = mybir.dt.float32
BF16 = mybir.dt.bfloat16
I32 = mybir.dt.int32
ds = bass.ds

P = 128
EPS = 1e-5
SHUT = -1e30
BIG = 3e38

K_PARTS = (3, 3, 2)
PAIRS = sum(K_PARTS)


def build(nc, x, ctx_in, mask, g_xattn, g_ffn, adj, Wq, bq, Wk, bk, Wv, bv, Wo, bo,
          gate_w, w1, b1, w2, b2, out):
    B, S, E = x.shape
    X, _, DFF = w1.shape
    D = P // PAIRS
    H = E // D
    QT = S // P
    EC = E // P
    FC = DFF // P
    TOK = B * S
    NT = TOK // P
    SLOTS = NT + X - 1
    SLOTS_R = SLOTS + SLOTS % 2
    HG = 4
    NG = H // HG
    QH = 2
    GROUPS = QH * NG
    QPG = QT // QH
    TPG = QPG * HG
    TILES = GROUPS * TPG
    HALF = S // QH
    VW = 32
    assert (D, H, E, S) == (16, 16, 256, 512)

    NB = 6
    NS = 3
    NTB = 2
    LT = 4
    LE = 4
    LP = LE + 1
    LO = LP + QT
    LAG = LO + 1
    DVE_COPIES = (1, 4)

    def dve_copies(n):
        return n // 8 * len(DVE_COPIES) + sum(1 for i in range(n % 8) if i in DVE_COPIES)

    def act_copies(n):
        return n - dve_copies(n)

    def before(n, bufs):
        t = n % TILES
        if t >= bufs:
            return n - bufs
        if n < TILES:
            return None
        return n - t - 1 - (TILES - 1 - t) % bufs

    SETUP = 6
    NEXT = 8
    TAIL_A = [(13, "heads", 0), (14, "heads", 1), (17, "turn", 0), (18, "turn", 1), (21, "out", 0),
              (22, "out", 1), (30, "normed", 0), (31, "normed", 1), (35, "gate", (0, 1)), (41, "rank", 0)]
    USES = sorted([(10, "values", 0), (11, "values", 1)] + TAIL_A
                  + [(24, "next x", 0), (25, "next x", 1), (27, "next ctx", 0), (28, "next ctx", 1),
                     (33, "next q", 0), (37, "next k", 0), (39, "next q", 1), (43, "next k", 1)]
                  + [(45, "heads", 2), (46, "heads", 3), (49, "turn", 2), (50, "turn", 3), (53, "out", 2),
                     (54, "out", 3), (60, "normed", 2), (61, "normed", 3), (64, "gate", (2,)),
                     (65, "gate", (3,))], key=lambda use: use[0])
    LAST_USES = [u for u in USES if not u[1].startswith("next")]
    NEXT_USES = [(k, w, a) for k, w, a in USES if w.startswith("next")]
    ACT_AT, VE_AT, ACT_QK_AT, VE_QK_AT = 0, 1, 0, 2
    ROW_STEPS = {26: 0, 27: 1, 56: 2, 57: 3}
    SHIFT_STEP, EXP_STEP, PICK_STEP = 36, 35, 38
    STATS_STEP, NORM_STEP = 15, 20
    assert min(USES)[0] >= LAG and max(USES)[0] + 3 < LAG + TILES
    PER = len(USES)
    LAST_SHIFT = len(LAST_USES) - PER
    assert PER % 2 == 0 and len(NEXT_USES) == NEXT

    def at_step(uses, n):
        return [(i, w, a) for i, (k, w, a) in enumerate(uses) if k == n]

    def ready(b, i):
        return b * PER + (SETUP + NEXT + i + 1)

    def free(b, i):
        return b * (PER // 2) + (SETUP + NEXT + i) // 2

    with ExitStack() as st:
        def sb(name, shape, dt=F32):
            return st.enter_context(nc.sbuf_tensor(name, shape, dt))

        def sem(name):
            return st.enter_context(nc.semaphore(name))

        w2s = sb("w2s", [P, X, FC, E])
        stack = w2s[:].rearrange("p x c e -> p (x c e)").bitcast(BF16).rearrange(
            "p (b t h s) -> p b t h s", b=2, t=2, h=H)
        pt = sb("pt", [P, 2, QT, HG, HALF])
        pt_flat = pt[:].rearrange("p a c j q -> p (a c j q)")
        wraw = pt_flat[:, 0:4 * EC * E].rearrange("p (w m e) -> p w m e", w=4, m=EC)
        w1s = pt_flat.rearrange("p (u k f) -> p u k f", u=4, k=EC)
        prob = sb("prob", [P, NB, S])
        negmax = sb("negmax", [P, NB])
        vals = sb("vals", [P, QT, H, VW])
        o_sb = sb("o_sb", [P, NG, QH, HALF])
        adjm = sb("adjm", [P, QT, S])
        maski = sb("maski", [P, QT, S], I32)
        xin = sb("xin", [P, QT, E])
        cin = sb("cin", [P, QT, E])
        xT = sb("xT", [P, EC, S])
        cT = sb("cT", [P, EC, S])
        parts = sb("parts", [P, 2, EC, 3, S], BF16)
        rest = sb("rest", [P, S])
        wT = sb("wT", [P, 4, EC, E])
        minus_half = sb("minus_half", [P, QT])
        ident = sb("ident", [P, P])
        stats = sb("stats", [P, QT, 6])
        mv = sb("mv", [P, QT, 2])
        rstd = sb("rstd", [P, QT])
        early = prob[:].rearrange("p n s -> p (n s)")
        zrow = early[0:1, 0:E]
        gate_r = early[0:X, 2 * E:3 * E]
        rowsm = early[0:X * FC + 2 * EC, 3 * E:3 * E + P]
        colsm = sb("colsm", [P, X * FC + 4])
        gateT = sb("gateT", [P, EC, X])
        bvb = sb("bvb", [P, E])
        bob = sb("bob", [P, E])
        gr = sb("gr", [P, 2])
        tg = sb("tg", [P, 2])
        logit = sb("logit", [P, QT, X])
        b1c = colsm[:, 0:X * FC]
        bqc = colsm[:, X * FC:X * FC + EC]
        bkc = colsm[:, X * FC + EC:X * FC + 2 * EC]
        rows = sb("rows", [P, 2, 2 * E])
        xres = sb("xres", [P, 2, E])
        attn = sb("attn", [P, 2, E])
        atT = sb("atT", [P, 2, EC, P])
        x2T = sb("x2T", [P, 2, EC, P])
        b2b = maski[:].rearrange("p t s -> p (t s)").bitcast(F32).rearrange("p (x e) -> p x e", x=X)
        hT = adjm[:].rearrange("p t s -> p (t s)").rearrange("p (u c t) -> p u c t", u=2, c=FC)
        xgT = xT[:].rearrange("p k (u t) -> p u k t", u=4)[:, 0:2]
        orow = cT[:, 0].rearrange("p (u e) -> p u e", u=2)
        ytmp = cT[:, 1].rearrange("p (u e) -> p u e", u=2)
        rinv = sb("rinv", [P, 2, H])
        st2 = sb("st2", [P, 2, 6])
        mv2 = sb("mv2", [P, 2, 2])
        rstd2 = sb("rstd2", [P, 2])
        ids = sb("ids", [P, B + 1, QT], I32)
        pair = sb("pair", [P, QT, 2], I32)
        posi = sb("posi", [P, QT], I32)
        empty = sb("empty", [P, TOK * X // P, 2], I32)
        slots = sb("slots", [P, SLOTS_R, 2], I32)
        eid = sb("eid", [P, SLOTS_R], I32)
        base_i = sb("base_i", [P, SLOTS_R], I32)
        gidx = sb("gidx", [P, 2], I32)
        xidx = sb("xidx", [P, 2], I32)
        sidx = sb("sidx", [P, 2], I32)
        ltri = sb("ltri", [P, P], BF16)
        ones = sb("ones", [P, P], BF16)
        onehot = sb("onehot", [P, QT, X], BF16)
        seven = sb("seven", [P, X])
        region = sb("region", [P, X])
        region0 = sb("region0", [P, X])
        thr = sb("thr", [P, NT])
        slotn = sb("slotn", [P, SLOTS_R])
        live = sb("live", [P, B + 1])
        dead = sb("dead", [P, B + 1])
        iot = sb("iot", [P, SLOTS_R], I32)
        key, place = (sb(n, [P, QT, X]) for n in ("key", "place"))
        mx, sm, em, km, wt, posf = (sb(n, [P, QT]) for n in ("mx", "sm", "em", "km", "wt", "posf"))
        cnt, tiles, end, end2, span = (sb(n, [P, X]) for n in ("cnt", "tiles", "end", "end2", "span"))
        cmp_t = sb("cmp_t", [P, X, NT])
        cmp_s = sb("cmp_s", [P, SLOTS_R, X])
        ef, bf = sb("ef", [P, SLOTS_R]), sb("bf", [P, SLOTS_R])

        bank = [st.enter_context(nc.psum_tensor(f"bank{i}", [P, 512], F32)) for i in range(8)]
        sc_bank, tr_bank, pv_bank, sp_bank = bank[0:NS], bank[NS:NS + NTB], bank[5], bank[6:8]

        part_d = nc.dram_tensor("part_d", [2, 2, 3, D, H, S], BF16, kind="Internal").ap()
        x1_d = nc.dram_tensor("x1_d", [TOK + 1, E], F32, kind="Internal").ap()
        xn_d = nc.dram_tensor("xn_d", [TOK + 1, E], F32, kind="Internal").ap()
        slot_d = nc.dram_tensor("slot_d", [X * TOK + P, 2], I32, kind="Internal").ap()

        x_v = x.rearrange("b (t p) e -> b p t e", p=P)
        c_v = ctx_in.rearrange("b (t p) e -> b p t e", p=P)
        m_v = mask.rearrange("b o (t p) s -> b p (o t) s", p=P)
        adj_v = adj.rearrange("(t p) s -> p t s", p=P)
        xt_v = x.rearrange("b (t p) e -> (b t) p e", p=P)
        out_v = out.rearrange("b s e -> (b s) e")
        w1_v = w1.rearrange("x (k p) f -> x p k f", p=P)

        (s_wraw, s_small, s_bcast, s_x, s_ctx, s_mask, s_const, s_m, s_stat, s_mv, s_rstd,
         s_xn, s_p0, s_rest, s_p1, s_parts, s_stack, s_adjm, s_penal, s_v, s_score,
         s_xT, s_masked, s_exp, s_trans, s_cact, s_cdve, s_pv, s_osb, s_tg, s_vinit, s_first) = [
            sem(n) for n in (
                "wraw", "small", "bcast", "x", "ctx", "mask", "const", "m", "stat", "mv",
                "rstd", "xn", "p0", "rest", "p1", "parts", "stack", "adjm", "penal", "v",
                "score", "xT", "masked", "exp", "trans", "cact", "cdve", "pv", "osb", "tg", "vinit", "first")]
        s_waited = [sem("waited0"), sem("waited1")]
        s_partd, s_adj, t_x, t_out = ([sem(f"{n}{k}") for k in range(2)]
                                      for n in ("partd", "adj", "t_xres", "t_out"))
        r_fill, f_free = sem("r_fill"), sem("f_free")
        s_eps, t_eps, s_half = sem("eps"), sem("t_eps"), sem("half")
        s_md = [sem("md0"), sem("md1")]
        (t_rinv, t_attn, t_atT, t_x1, t_stat, t_mv, t_rstd, t_row, t_x2T, t_rowfree, r_dve, t_ones) = [
            sem("t_" + n) for n in (
                "rinv", "attn", "atT", "x1", "stat", "mv", "rstd", "row", "x2T", "rowfree", "r_dve", "ones")]
        (r_exp, r_sub, r_oh, r_pair, r_scat, r_free, r_ids, r_init, r_eid, r_w2,
         r_b2, r_mx, r_st, r_wt) = [sem("r_" + n) for n in (
             "exp", "sub", "oh", "pair", "scat", "free", "ids", "init", "eid",
             "w2", "b2", "mx", "st", "wt")]
        r_slots = [sem("r_slots0"), sem("r_slots1")]
        (f_xt, f_xgT, f_h, f_hT, f_y, f_tmp, f_out, f_gi, f_xi, f_si) = [
            sem("f_" + n) for n in ("xt", "xgT", "h", "hT", "y", "tmp", "out", "gi", "xi", "si")]
        f_w1 = [sem("f_w1_0"), sem("f_w1_1")]
        f_row = [sem("f_row0"), sem("f_row1")]
        f_x1 = [sem("f_x1_0"), sem("f_x1_1")]
        f_sc = [sem("f_sc0"), sem("f_sc1")]

        block = st.enter_context(nc.Block())

        def wait_apart(eng, s, value):
            eng.wait_ge(s, value)
            eng.sem_inc(s_waited[eng is nc.vector], 1)

        STACKED = 16 * 2 * len(K_PARTS)

        def tile_of(n):
            g, r = divmod(n % TILES, TPG)
            qh, hg = divmod(g, NG)
            q2, j = divmod(r, HG)
            return g, qh * QPG + q2, q2, hg * HG + j, j

        @block.sync
        def _(sp):
            sp.dma_start(xin[:], x_v[0]).then_inc(s_x, 16)
            for n, w in enumerate((Wq, Wk, Wv, Wo)):
                sp.dma_start(wraw[:, n], w.rearrange("(m p) e -> p m e", p=P)).then_inc(s_wraw, 16)
            sp.dma_start(cin[:], c_v[0]).then_inc(s_ctx, 16)
            sp.dma_start(rowsm[0:X * FC, :], b1.rearrange("x (c p) -> (x c) p", p=P)).then_inc(s_small, 16)
            sp.dma_start(rowsm[X * FC:X * FC + EC, :], bq.rearrange("(c p) -> c p", p=P)).then_inc(s_small, 16)
            sp.dma_start(rowsm[X * FC + EC:X * FC + 2 * EC, :], bk.rearrange("(c p) -> c p", p=P)).then_inc(s_small, 16)
            sp.dma_start(gate_r, gate_w).then_inc(s_small, 16)
            sp.dma_start(maski[:], m_v[0]).then_inc(s_mask, 16)

            def load_adj(q0, q1):
                sp.dma_start(adjm[:, q0:q1], adj_v[:, q0:q1]).then_inc(s_adj[q0 > 0], 16)

            load_adj(0, QT // 2)
            load_adj(QT // 2, QT)
            for dst, src in ((bvb[:], bv), (bob[:], bo)):
                sp.dma_start(dst, src.rearrange("(o e) -> o e", o=1).to_broadcast([P, E])).then_inc(s_bcast, 16)
            for n, g in enumerate((g_xattn, g_ffn)):
                sp.dma_start(gr[:, n:n + 1], g.rearrange("(o e) -> o e", o=1).to_broadcast([P, 1])).then_inc(s_bcast, 16)

            def part_out(b, par, m, t):
                sp.wait_ge(s_parts, b * 4 + (2 * m + t + 1))
                for a in range(3):
                    sp.dma_start(part_d[par, t, a, :, m * (H // EC):(m + 1) * (H // EC)].rearrange(
                        "o d h s -> (o h) d s"), parts[:, t, m, a]).then_inc(s_partd[t], 16)

            def stack_in(par, t, h0, h1, done):
                at = 0
                for part, n in enumerate(K_PARTS):
                    if t == 0:
                        src = part_d[par, t, part, :, h0:h1].rearrange(
                            "o d h s -> o d (h s)").to_broadcast([n, D, (h1 - h0) * S])
                    else:
                        src = part_d[par, t, 0:n, :, h0:h1].rearrange("o a d h s -> (o a) d (h s)")
                    sp.dma_start(stack[D * at:D * (at + n), par, t, h0:h1].rearrange(
                        "p o h s -> p (o h s)"), src).then_inc(done, 16)
                    at += n

            def stack_parts(b, par):
                for m in range(EC):
                    for t in range(2):
                        part_out(b, par, m, t)
                for t in range(2):
                    sp.wait_ge(s_partd[t], b * 96 + 96)
                    stack_in(par, t, 0, H, s_stack)

            for m in range(EC):
                for t in range(2):
                    part_out(0, ds(0, 1), m, t)
                for t in range(2):
                    sp.wait_ge(s_partd[t], 48 * (m + 1))
                    stack_in(ds(0, 1), t, m * H // EC, (m + 1) * H // EC, (s_first, s_stack)[m])

            def load_xres(t, u):
                sp.dma_start(xres[:, u], xt_v[ds(t, 1)].rearrange("b p e -> p (b e)")).then_inc(t_x[u], 16)

            def tail_pair(b, t, k, nxt):
                for u in range(2):
                    sp.wait_ge(t_x1, b * 4 + k + u + 1)
                    if nxt is not None:
                        load_xres(nxt + u, u)
                for u in range(2):
                    sp.wait_ge(t_row, b * 4 + k + u + 1)
                    sp.dma_start(x1_d[ds((t + u) * P, P), :], rows[:, u, 0:E]).then_inc(t_out[u], 16)
                    sp.dma_start(xn_d[ds((t + u) * P, P), :], rows[:, u, E:2 * E]).then_inc(t_out[u], 16)
                for u in range(2):
                    sp.wait_ge(t_out[u], b * 64 + (16 * k + 32))
                    sp.wait_ge(t_x2T, b * 4 + k + u + 1)
                    sp.sem_inc(t_rowfree, 1)

            for u in range(2):
                load_xres(NT - 2 + u, u)
            with sp.Fori(0, B - 1) as b:
                sp.wait_ge(s_p0, b * 4 + 4)
                sp.dma_start(xin[:], x_v[ds(b + 1, 1)].rearrange("b p t e -> p (b t) e")).then_inc(s_x, 16)
                sp.dma_start(cin[:], c_v[ds(b + 1, 1)].rearrange("b p t e -> p (b t) e")).then_inc(s_ctx, 16)
                sp.wait_ge(s_adjm, b * QT + QT)
                sp.dma_start(maski[:], m_v[ds(b + 1, 1)].rearrange("b p t e -> p (b t) e")).then_inc(s_mask, 16)
                tail_pair(b, (b * QT + (NT - 2)) % NT, 0, b * QT)
                sp.wait_ge(s_masked, b * TILES + TILES // 2)
                load_adj(0, QT // 2)
                stack_parts(b + 1, ds((b + 1) % 2, 1))
                tail_pair(b, b * QT, 2, b * QT + 2)
                sp.wait_ge(s_masked, b * TILES + TILES)
                load_adj(QT // 2, QT)

            def load_w2(e):
                sp.dma_start(w2s[:, e], w2[e].rearrange("(c p) f -> p c f", p=P)).then_inc(r_w2, 16)

            last = B - 1
            tail_pair(last, last * QT - 2, 0, last * QT)
            sp.wait_ge(s_score, last * TILES)
            for e in range(X // 2):
                load_w2(e)
            tail_pair(last, last * QT, 2, last * QT + 2)
            sp.wait_ge(s_adjm, B * QT)
            sp.dma_start(b2b, b2.rearrange("(o x) e -> o (x e)", o=1).to_broadcast([P, X * E]).rearrange(
                "p (x e) -> p x e", x=X)).then_inc(r_b2, 16)
            sp.wait_ge(s_score, B * TILES)
            for e in range(X // 2, X):
                load_w2(e)
            tail_pair(B, NT - 2, 0, None)
            sp.wait_ge(r_eid, 1)

            def load_slots(s, u, after=None):
                at = sp.value_load(base_i[0:1, ds(s, 1)], min_val=0, max_val=X * TOK)
                if after is not None:
                    sp.wait_ge(f_xt, after)
                sp.dma_start(slots[:, ds(s, 1), :].rearrange("p s a -> p (s a)"),
                             slot_d[ds(at, P), :]).then_inc(r_slots[u], 16)

            def load_w1(s, u, after=None):
                e = sp.value_load(eid[0:1, ds(s, 1)], min_val=0, max_val=X - 1)
                if after is not None:
                    sp.wait_ge(f_h, FC * after)
                sp.dma_start(w1s[:, u], w1_v[ds(e, 1)].rearrange("x p k f -> p (x k) f")).then_inc(f_w1[u], 16)

            load_w1(0, 0)
            sp.wait_ge(r_free, B + 2)
            for u in range(2):
                load_slots(u, u)
            load_w1(1, 1)
            with sp.Fori(0, (SLOTS - 3) // 2) as i:
                for u in range(2):
                    load_slots(i * 2 + (u + 2), u, i * 2 + u + 1)
                    load_w1(i * 2 + (u + 2), u, i * 2 + u + 1)
            load_slots(SLOTS - 1, 0, SLOTS - 2)
            load_w1(SLOTS - 1, 0, SLOTS - 2)
            for u in range(2):
                sp.wait_ge(f_sc[u], 16 * ((SLOTS + 1 - u) // 2))

        @block.gpsimd
        def _(po):
            po.memset(ident[:], 0.0).then_inc(s_const, 1)
            po.memset(ones[:], 1.0).then_inc(s_const, 1)
            po.memset(minus_half[:], -0.5).then_inc(s_half, 1)
            po.memset(vals[:], 0.0).then_inc(s_vinit, 1)
            po.wait_ge(s_const, 2)
            po.affine_select(out=ident[:], in_=ident[:], compare_op=ALU.not_equal, fill=1.0, base=0,
                             pattern=[[-1, P]], channel_multiplier=1).then_inc(s_const, 1)
            po.wait_ge(s_vinit, 1)
            po.memset(vals[:, :, :, D:D + 1], 1.0).then_inc(s_vinit, 1)
            po.affine_select(out=ltri[:], in_=ones[:], compare_op=ALU.is_gt, fill=0.0, base=0,
                             pattern=[[1, P]], channel_multiplier=-1).then_inc(s_const, 1)
            po.iota(ids[:].rearrange("p b t -> p (b t)"), pattern=[[P, (B + 1) * QT]], base=-S,
                    channel_multiplier=1).then_inc(s_const, 1)
            n = 5

            def numbers(dst, width, step, base):
                nonlocal n
                po.wait_ge(s_const, n)
                po.iota(iot[:, 0:width], pattern=[[step, width]], base=base,
                        channel_multiplier=0).then_inc(s_const, 1)
                po.wait_ge(s_const, n + 1)
                po.tensor_copy(dst, iot[:, 0:width]).then_inc(s_const, 1)
                n += 2

            numbers(seven[:], X, -1, X)
            numbers(region[:], X, TOK, 0)
            numbers(region0[:], X, TOK, 0)
            numbers(thr[:], NT, P, 0)
            numbers(slotn[:], SLOTS_R, 1, 0)
            po.memset(live[:, 0:1], 0.0).then_inc(s_const, 1)
            po.memset(live[:, 1:], 1.0).then_inc(s_const, 1)
            po.memset(dead[:, 0:1], 1e6).then_inc(s_const, 1)
            po.memset(dead[:, 1:], 0.0).then_inc(s_const, 1)
            po.memset(o_sb[:, :, 1, :], 1.0).then_inc(t_ones, 1)
            po.memset(logit[:], 0.0).then_inc(t_ones, 1)
            po.memset(empty[:, :, 0], TOK).then_inc(r_init, 1)
            po.memset(empty[:, :, 1], 0).then_inc(r_init, 1)
            po.memset(zrow, 0.0).then_inc(r_init, 1)
            po.wait_ge(r_init, 3)
            po.dma_start(slot_d[0:X * TOK].rearrange("(p s) a -> p s a", p=P), empty[:]).then_inc(r_fill, 16)
            po.dma_start(slot_d[X * TOK:], empty[:, 0]).then_inc(r_fill, 16)
            for d in (x1_d, xn_d):
                po.dma_start(d[TOK:TOK + 1, :], zrow).then_inc(r_fill, 16)

            def masks(b, q0, q1):
                wait_apart(po, s_adj[q0 > 0], b * 16 + 16)
                for qt in range(q0, q1):
                    mf = maski[:, qt].bitcast(F32)
                    po.tensor_scalar(mf, maski[:, qt], 0.0, SHUT, ALU.is_equal, ALU.mult).then_inc(s_penal, 1)
                    po.wait_ge(s_penal, b * QT + qt + 1)
                    po.tensor_tensor(adjm[:, qt], mf, adjm[:, qt], ALU.add).then_inc(s_adjm, 1)

            def norm(b):
                wait_apart(po, s_mv, b * QT + QT)
                po.tensor_scalar(mv[:, :, 1], mv[:, :, 1], EPS, None, ALU.add).then_inc(s_eps, 1)
                po.wait_ge(s_eps, b + 1)
                po.tensor_tensor(rstd[:], mv[:, :, 1], minus_half[:], ALU.pow).then_inc(s_rstd, 1)

            def split(b, i, t, m, nxt):
                k = 2 * m + t + 1
                wait_apart(po, s_md[i % 2], free(b, i) + 1)
                po.tensor_copy(parts[:, t, m, 1], rest[:]).then_inc(s_p1, 1)
                po.wait_ge(s_p1, nxt * 4 + k)
                po.tensor_tensor(parts[:, t, m, 2], rest[:], parts[:, t, m, 1], ALU.subtract).then_inc(s_parts, 1)

            def splits(b, uses, nxt):
                for i, what, k in uses:
                    if what in ("next q", "next k"):
                        split(b, i, int(what == "next k"), k, nxt)

            po.wait_ge(s_half, 1)
            norm(0)
            po.wait_ge(s_mask, 16)
            masks(0, 0, QT // 2)
            masks(0, QT // 2, QT)

            def tail_rstd(b, k):
                for u in range(2):
                    wait_apart(po, t_mv, b * 4 + k + u + 1)
                    po.tensor_scalar(mv2[:, u, 1:2], mv2[:, u, 1:2], EPS, None, ALU.add).then_inc(t_eps, 1)
                    po.wait_ge(t_eps, b * 4 + k + u + 1)
                    po.tensor_tensor(rstd2[:, u:u + 1], mv2[:, u, 1:2], minus_half[:, 0:1],
                                     ALU.pow).then_inc(t_rstd, 1)

            def to_slots(b):
                po.tensor_copy(pair[:, :, 0], ids[:, ds(b, 1), :].rearrange("p b t -> p (b t)")).then_inc(r_ids, 1)
                po.wait_ge(r_ids, b + 1)
                po.wait_ge(r_wt, b + 1)
                wait_apart(po, r_pair, b + 1)
                for t in range(QT):
                    po.indirect_dma_start(slot_d, bass.IndirectOffsetOnAxis(ap=posi[:, t:t + 1], axis=0),
                                          pair[:, t], None, bounds_check=X * TOK - 1,
                                          oob_is_err=False).then_inc(r_scat, 16)
                po.wait_ge(r_scat, b * (16 * QT) + 16 * QT)
                po.sem_inc(r_free, 1)

            po.wait_ge(r_fill, 64)
            with po.Fori(0, B - 1) as b:
                norm(b + 1)
                tail_rstd(b, 0)
                splits(b, [(i, what, k) for i, (n, what, k) in enumerate(USES)], b + 1)
                to_slots(b)
                tail_rstd(b, 2)
                wait_apart(po, s_mask, b * 16 + 32)
                masks(b + 1, 0, QT // 2)
                masks(b + 1, QT // 2, QT)
            tail_rstd(B - 1, 0)
            to_slots(B - 1)
            tail_rstd(B - 1, 2)
            tail_rstd(B, 0)
            to_slots(B)

            def gather_normed(s, i, u):
                wait_apart(po, r_slots[u], i * 16 + 16)
                po.tensor_copy(gidx[:, u:u + 1], slots[:, ds(s, 1), 0]).then_inc(f_gi, 1)
                wait_apart(po, f_gi, s + 1)
                po.indirect_dma_start(rows[:, u, E:2 * E], None, xn_d,
                                      bass.IndirectOffsetOnAxis(ap=gidx[:, u:u + 1], axis=0)
                                      ).then_inc(f_row[u], 16)

            def gather_x(s, i, u):
                po.tensor_copy(xidx[:, u:u + 1], slots[:, ds(s, 1), 0]).then_inc(f_xi, 1)
                wait_apart(po, f_xi, s + 1)
                po.indirect_dma_start(rows[:, u, 0:E], None, x1_d,
                                      bass.IndirectOffsetOnAxis(ap=xidx[:, u:u + 1], axis=0)
                                      ).then_inc(f_x1[u], 16)

            def scatter(s, u):
                po.tensor_copy(sidx[:, u:u + 1], slots[:, ds(s, 1), 0]).then_inc(f_si, 1)
                wait_apart(po, f_si, s + 1)
                po.indirect_dma_start(out_v, bass.IndirectOffsetOnAxis(ap=sidx[:, u:u + 1], axis=0),
                                      orow[:, u], None, bounds_check=TOK - 1,
                                      oob_is_err=False).then_inc(f_sc[u], 16)

            def scattered(i, u):
                po.wait_ge(f_sc[u], i * 16 + 16)
                po.sem_inc(f_free, 1)

            for u in range(2):
                gather_normed(u, 0, u)
            for u in range(2):
                gather_x(u, 0, u)

            def hand_on(s, i, u, gi, first=False, more=True):
                if more:
                    wait_apart(po, f_xt, s + 1)
                    gather_normed(s + 2, gi, u)
                if not first:
                    scattered(i, 1 - u)
                wait_apart(po, f_out, s + 1)
                if more:
                    gather_x(s + 2, gi, u)
                scatter(s, u)

            hand_on(0, 0, 0, 1, first=True)
            with po.Fori(0, (SLOTS - 3) // 2) as i:
                hand_on(i * 2 + 1, i, 1, i + 1)
                hand_on(i * 2 + 2, i, 0, i + 2)
            for s in range(SLOTS - 2, SLOTS):
                hand_on(s, (s - 1) // 2, s % 2, None, more=False)

        @block.tensor
        def _(pe):
            def bank_free(b, i):
                k = SETUP + NEXT + i
                if not isinstance(b, int) or b > 0 or k >= 2:
                    pe.wait_ge(s_md[k % 2], free(b, i))
                return sp_bank[k % 2]

            pe.wait_ge(s_const, 3)
            pe.wait_ge(s_wraw, 64)
            for w in range(4):
                bank_free(0, w - SETUP - NEXT)
                for k in range(EC):
                    for m in range(EC):
                        mm = pe.transpose(sp_bank[w % 2][:, k * E + m * P:k * E + (m + 1) * P],
                                          wraw[:, w, m, k * P:(k + 1) * P], ident[:])
                mm.then_inc(s_m, 1)
            pe.wait_ge(s_small, 64)
            bank_free(0, 4 - SETUP - NEXT)
            nr = X * FC + 2 * EC
            pe.transpose(sp_bank[0][:, 0:nr], rowsm, ident[0:nr, 0:nr]).then_inc(s_m, 1)
            bank_free(0, 5 - SETUP - NEXT)
            for k in range(EC):
                mm = pe.transpose(sp_bank[1][:, k * X:(k + 1) * X], gate_r[:, k * P:(k + 1) * P],
                                  ident[0:X, 0:X])
            mm.then_inc(s_m, 1)

            def turn_in(b, i, src, k):
                o = bank_free(b, i)
                for t in range(QT):
                    mm = pe.transpose(o[:, t * P:(t + 1) * P], src[:, t, k * P:(k + 1) * P], ident[:])
                mm.then_inc(s_m, 1)

            def project(b, i, w, src, m, k):
                o = bank_free(b, i) if k == 0 else sp_bank[i % 2]
                mm = pe.matmul(o[:], wT[:, w, k, m * P:(m + 1) * P], src[:, k],
                               start=k == 0, stop=k == EC - 1)
                if k == EC - 1:
                    mm.then_inc(s_m, 1)

            def next_use(b, i, what, k, nxt):
                if what == "next x":
                    if k == 0:
                        pe.wait_ge(s_xn, nxt * QT + QT)
                    turn_in(b, i, xin, k)
                if what == "next ctx":
                    if k == 0:
                        pe.wait_ge(s_ctx, nxt * 16 + 16)
                    turn_in(b, i, cin, k)
                if what == "next q":
                    if k == 0:
                        pe.wait_ge(s_xT, nxt * 4 + 2)
                    project(b, i, 0, xT, k, 0)
                if what == "next k":
                    if k == 0:
                        pe.wait_ge(s_xT, nxt * 4 + 4)
                    project(b, i, 1, cT, k, 0)

            def next_rest(b, i, what, k):
                if what == "next q":
                    project(b, i, 0, xT, k, 1)
                if what == "next k":
                    project(b, i, 1, cT, k, 1)

            def values(b, i, h):
                o = bank_free(b, i)
                for t in range(2):
                    for k in range(EC):
                        mm = pe.matmul(o[:, t * E:(t + 1) * E], cT[:, k, (2 * h + t) * P:(2 * h + t + 1) * P],
                                       wT[:, 2, k], start=k == 0, stop=k == EC - 1)
                mm.then_inc(s_m, 1)

            def tail_use(b, i, what, k):
                if what == "rank":
                    pe.wait_ge(r_oh, b + 1)
                    o = bank_free(b, i)
                    for t in range(QT):
                        pe.matmul(o[:, QT * X:(QT + 1) * X], ones[:], onehot[:, t], start=t == 0,
                                  stop=t == QT - 1)
                    pe.matmul(o[:, 0:QT * X], ltri[:], onehot[:].rearrange("p t x -> p (t x)"), start=True,
                              stop=False)
                    for t in range(QT - 1):
                        for t2 in range(t + 1, QT):
                            mm = pe.matmul(o[:, t2 * X:(t2 + 1) * X], ones[:], onehot[:, t], start=False,
                                           stop=t == QT - 2)
                    mm.then_inc(s_m, 1)
                    return
                if what == "gate":
                    pe.wait_ge(t_x2T, b * 4 + k[-1] + 1)
                    o = bank_free(b, i)
                    for j, kk in enumerate(k):
                        for c in range(EC):
                            mm = pe.matmul(o[:, j * X:(j + 1) * X], x2T[:, kk % 2, c], gateT[:, c],
                                           start=c == 0, stop=c == EC - 1)
                    mm.then_inc(s_m, 1)
                    return
                u = k % 2
                if what == "heads":
                    o = bank_free(b, i)
                    for a in range(NG):
                        mm = pe.transpose(o[:, a * P:(a + 1) * P], o_sb[:, a, int(k < 2), u * P:(u + 1) * P],
                                          ident[:])
                if what == "turn":
                    pe.wait_ge(t_attn, b * 4 + k + 1)
                    o = bank_free(b, i)
                    for c in range(EC):
                        mm = pe.transpose(o[:, c * P:(c + 1) * P], attn[:, u, c * P:(c + 1) * P], ident[:])
                if what == "out":
                    pe.wait_ge(t_atT, b * 4 + k + 1)
                    o = bank_free(b, i)
                    for c in range(EC):
                        mm = pe.matmul(o[:, 0:E], atT[:, u, c], wT[:, 3, c], start=c == 0, stop=c == EC - 1)
                if what == "normed":
                    pe.wait_ge(t_row, b * 4 + k + 1)
                    o = bank_free(b, i)
                    for c in range(EC):
                        mm = pe.transpose(o[:, c * P:(c + 1) * P], rows[:, u, E + c * P:E + (c + 1) * P],
                                          ident[:])
                mm.then_inc(s_m, 1)

            def scores(b, par, n):
                g, qt, q2, h, j = tile_of(n)
                m = n % TILES % NS
                if before(n, NS) is not None:
                    pe.wait_ge(s_masked, b * TILES + (before(n, NS) + 1))
                q = stack[:, par, 0, h, qt * P:(qt + 1) * P].rearrange("p o q -> p (o q)")
                k = stack[:, par, 1, h, :].rearrange("p o q -> p (o q)")
                pe.matmul(sc_bank[m][:], q, k, start=True, stop=True).then_inc(s_score, 1)

            def transposes(b, n):
                pe.wait_ge(s_exp, b * TILES + n + 1)
                if n >= NTB:
                    if (n - NTB) % 8 in DVE_COPIES:
                        pe.wait_ge(s_cdve, b * dve_copies(TILES) + dve_copies(n - NTB + 1))
                    else:
                        pe.wait_ge(s_cact, b * act_copies(TILES) + act_copies(n - NTB + 1))
                for c in range(QT):
                    mm = pe.transpose(tr_bank[n % NTB][:, c * P:(c + 1) * P], prob[:, n % TILES % NB, c * P:(c + 1) * P],
                                      ident[:])
                mm.then_inc(s_trans, 1)

            def weigh(b, g, c):
                if c == 0:
                    pe.wait_ge(s_cact, b * act_copies(TILES) + act_copies(TPG * (g + 1)))
                    pe.wait_ge(s_cdve, b * dve_copies(TILES) + dve_copies(TPG * (g + 1)))
                    pe.wait_ge(s_osb, b * GROUPS + (g + 2))
                hg = g % NG
                for j in range(HG):
                    mm = pe.matmul(pv_bank[32 * j:32 * j + 32, (g % 2) * HALF:(g % 2 + 1) * HALF],
                                   vals[:, c, hg * HG + j, :], pt[:, g % 2, c, j, :],
                                   start=c == 0, stop=c == QT - 1)
                if c == QT - 1:
                    mm.then_inc(s_pv, 1)

            def step(b, n, uses, last=False):
                if n < TILES or not last:
                    if n == 0:
                        pe.wait_ge(s_first, STACKED)
                    if n in (2 * TPG, TILES):
                        pe.wait_ge(s_stack, b * STACKED + (n // TILES + 1) * STACKED)
                    scores(b, ds((b + n // TILES) % 2, 1), n)
                if LT <= n and (n < TILES + LT or not last):
                    transposes(b, n - LT)
                if n >= LP + TPG and (n - LP) % TPG < QT:
                    g, c = divmod(n - LP - TPG, TPG)
                    if g == 0 and c == 0:
                        pe.wait_ge(s_v, b * 2 + 2)
                    weigh(b, g, c)
                for i, what, k in at_step(uses, n - 1):
                    if what.startswith("next"):
                        next_rest(b, i, what, k)
                for i, what, k in at_step(uses, n):
                    if what == "heads" and k == 2:
                        pe.wait_ge(s_osb, b * GROUPS + (NG + 2))
                    if what == "values":
                        values(b, i, k)
                    elif what.startswith("next"):
                        next_use(b, i, what, k, b + 1)
                    else:
                        tail_use(b, i, what, k)

            for j, (n, what, k) in enumerate(NEXT_USES):
                next_use(0, j - NEXT, what, k, 0)
                next_rest(0, j - NEXT, what, k)
            pe.wait_ge(t_ones, 2)
            for n in range(LAG):
                step(0, n, USES)
            with pe.Fori(0, B - 1) as b:
                for n in range(LAG, LAG + TILES):
                    step(b, n, USES)
            for n in range(LAG, LO + TILES):
                step(B - 1, n, LAST_USES, True)
            pe.wait_ge(s_osb, B * GROUPS + 2)
            for i, (n, what, k) in enumerate(TAIL_A):
                tail_use(B, i + LAST_SHIFT, what, k)

            def turn_rows(i, u):
                pe.wait_ge(f_row[u], i * 16 + 16)
                for k in range(EC):
                    mm = pe.transpose(bank[4 * u][:, k * P:(k + 1) * P], rows[:, u, E + k * P:E + (k + 1) * P],
                                      ident[:])
                mm.then_inc(f_xt, 1)

            def expert(s, i, u, last=False):
                e = pe.value_load(eid[0:1, ds(s, 1)], min_val=0, max_val=X - 1)
                pe.wait_ge(f_w1[u], i * 16 + 16)
                pe.wait_ge(f_xgT, s + 1)
                for c in range(FC):
                    o = bank[4 * u + 1 + c // 4][:, (c % 4) * P:(c % 4 + 1) * P]
                    for k in range(EC):
                        mm = pe.matmul(o, w1s[:, u, k, c * P:(c + 1) * P], xgT[:, u, k],
                                       start=k == 0, stop=k == EC - 1)
                    mm.then_inc(f_h, 1)
                if not last:
                    turn_rows(i + u, 1 - u)
                pe.wait_ge(f_tmp, s + 1)
                for c in range(FC):
                    pe.wait_ge(f_hT, s * FC + c + 1)
                    mm = pe.matmul(bank[4 * u + 3][:, 0:E], hT[:, u, c],
                                   w2s[:, ds(e, 1), c, :].rearrange("p x e -> p (x e)"),
                                   start=c == 0, stop=c == FC - 1)
                mm.then_inc(f_y, 1)

            pe.wait_ge(r_eid, 1)
            pe.wait_ge(r_w2, 16 * X)
            turn_rows(0, 0)
            with pe.Fori(0, SLOTS // 2) as i:
                for u in range(2):
                    expert(i * 2 + u, i, u)
            expert(SLOTS - 1, SLOTS // 2, 0, True)

        @block.scalar
        def _(act):
            for w in range(4):
                act.wait_ge(s_m, w + 1)
                act.activation(wT[:, w], sp_bank[w % 2][:].rearrange("p (k f) -> p k f", k=EC), ACT.Copy,
                               scale=float(D) ** -0.5 if w == 0 else 1.0).then_inc(s_md[w % 2], 1)
            act.wait_ge(s_m, 5)
            act.activation(colsm[:], sp_bank[0][:, 0:X * FC + 2 * EC], ACT.Copy).then_inc(s_tg, 1)
            act.wait_ge(s_tg, 1)
            act.activation(bqc, bqc, ACT.Copy, scale=float(D) ** -0.5).then_inc(s_md[0], 1)
            act.wait_ge(s_m, 6)
            act.activation(gateT[:].rearrange("p k x -> p (k x)"), sp_bank[1][:, 0:EC * X],
                           ACT.Copy).then_inc(s_md[1], 1)
            act.wait_ge(s_md[0], 3)

            def next_use(b, i, what, k, nxt):
                o = sp_bank[i % 2]
                act.wait_ge(s_m, ready(b, i))
                if what in ("next x", "next ctx"):
                    dst = xT if what == "next x" else cT
                    act.activation(dst[:, k], o[:], ACT.Copy).then_inc(s_xT, 1)
                    act.wait_ge(s_xT, nxt * 4 + (1 if what == "next x" else 3) + k)
                    act.sem_inc(s_md[i % 2], 1)
                else:
                    t = int(what == "next k")
                    if not (isinstance(nxt, int) and nxt == 0):
                        act.wait_ge(s_partd[t], nxt * 96)
                    act.activation(parts[:, t, k, 0], o[:], ACT.Identity,
                                   bias=(bqc, bkc)[t][:, k:k + 1]).then_inc(s_p0, 1)

            def tail_use(b, i, what, k):
                if what not in ("turn", "normed"):
                    return
                act.wait_ge(s_m, ready(b, i))
                dst, done = (atT, t_atT) if what == "turn" else (x2T, t_x2T)
                act.activation(dst[:, k % 2], sp_bank[i % 2][:, 0:E].rearrange("p (k q) -> p k q", k=EC),
                               ACT.Copy).then_inc(done, 1)
                act.wait_ge(done, b * 4 + k + 1)
                act.sem_inc(s_md[i % 2], 1)

            def route_exp(b):
                act.wait_ge(r_sub, b + 1)
                act.activation(logit[:], logit[:], ACT.Exp).then_inc(r_exp, 1)

            def step(b, n, uses, last=False):
                c = n - LE
                if 0 <= c and (c < TILES or not last) and c % 8 not in DVE_COPIES:
                    g, qt, q2, h, j = tile_of(c)
                    act.wait_ge(s_trans, b * TILES + c + 1)
                    if c >= 2 * TPG:
                        act.wait_ge(s_pv, b * GROUPS + (c // TPG - 1))
                    act.activation(pt[:, g % 2, :, j, q2 * P:(q2 + 1) * P],
                                   tr_bank[c % NTB][:].rearrange("p (c q) -> p c q", c=QT),
                                   ACT.Copy).then_inc(s_cact, 1)
                if n < TILES or not last:
                    m = n % TILES % NB
                    act.wait_ge(s_masked, b * TILES + n + 1)
                    act.activation(prob[:, m], prob[:, m], ACT.Exp, scale=-1.0,
                                   bias=negmax[:, m:m + 1]).then_inc(s_exp, 1)
                for i, what, k in at_step(uses, n - ACT_AT):
                    if what in ("next x", "next ctx"):
                        next_use(b, i, what, k, b + 1)
                    elif not what.startswith("next"):
                        tail_use(b, i, what, k)
                for i, what, k in at_step(uses, n - ACT_QK_AT):
                    if what in ("next q", "next k"):
                        next_use(b, i, what, k, b + 1)
                if n == EXP_STEP:
                    route_exp(b)

            for j, (n, what, k) in enumerate(NEXT_USES):
                next_use(0, j - NEXT, what, k, 0)
            act.wait_ge(s_bcast, 64)
            act.activation(tg[:], gr[:], ACT.Tanh).then_inc(s_tg, 1)
            for n in range(LAG):
                step(0, n, USES)
            with act.Fori(0, B - 1) as b:
                for n in range(LAG, LAG + TILES):
                    step(b, n, USES)
            for n in range(LAG, LO + TILES):
                step(B - 1, n, LAST_USES, True)
            for i, (n, what, k) in enumerate(TAIL_A):
                tail_use(B, i + LAST_SHIFT, what, k)
            route_exp(B)

            def turned_rows(s, u):
                act.wait_ge(f_xt, s + 1)
                act.activation(xgT[:, u], bank[4 * u][:, 0:E].rearrange("p (k q) -> p k q", k=EC),
                               ACT.Copy).then_inc(f_xgT, 1)

            def expert(s, i, u, last=False):
                e = act.value_load(eid[0:1, ds(s, 1)], min_val=0, max_val=X - 1)
                for c in range(FC):
                    if c % 4 == 0:
                        act.wait_ge(f_h, s * FC + c + 4)
                    act.activation(hT[:, u, c], bank[4 * u + 1 + c // 4][:, (c % 4) * P:(c % 4 + 1) * P],
                                   ACT.Relu, bias=b1c[:, ds(e * FC + c, 1)]).then_inc(f_hT, 1)
                if not last:
                    turned_rows(s + 1, 1 - u)

            act.wait_ge(r_eid, 1)
            turned_rows(0, 0)
            with act.Fori(0, SLOTS // 2) as i:
                for u in range(2):
                    expert(i * 2 + u, i, u)
            expert(SLOTS - 1, SLOTS // 2, 0, True)

        @block.vector
        def _(ve):
            def norm_stats(b):
                ve.wait_ge(s_x, b * 16 + 16)
                for t in range(QT):
                    ve.bn_stats(stats[:, t], xin[:, t]).then_inc(s_stat, 1)
                for t in range(QT):
                    wait_apart(ve, s_stat, b * QT + t + 1)
                    ve.bn_aggr(mv[:, t], stats[:, t]).then_inc(s_mv, 1)

            def norm(b):
                ve.wait_ge(s_rstd, b + 1)
                for t in range(QT):
                    ve.tensor_scalar(xin[:, t], xin[:, t], mv[:, t, 0:1], rstd[:, t:t + 1],
                                     ALU.subtract, ALU.mult).then_inc(s_xn, 1)

            def next_use(b, i, what, m, nxt):
                if what not in ("next q", "next k"):
                    return
                t = int(what == "next k")
                k = 2 * m + t + 1
                ve.wait_ge(s_p0, nxt * 4 + k)
                if not isinstance(nxt, int) or k > 1:
                    ve.wait_ge(s_parts, nxt * 4 + (k - 1))
                ve.scalar_tensor_tensor(out=rest[:], in0=sp_bank[i % 2][:], scalar=(bqc, bkc)[t][:, m:m + 1],
                                        in1=parts[:, t, m, 0], op0=ALU.add, op1=ALU.subtract
                                        ).then_inc(s_md[i % 2], 1)

            def values(b, i, h):
                ve.wait_ge(s_m, ready(b, i))
                for t in range(2):
                    ins = ve.tensor_tensor(vals[:, 2 * h + t, :, 0:D],
                                           sp_bank[i % 2][:, t * E:(t + 1) * E].rearrange("p (h d) -> p h d", d=D),
                                           bvb[:].rearrange("p (h d) -> p h d", d=D), ALU.add)
                    ins.then_inc((s_rest, s_v)[t], 1)
                ve.wait_ge(s_v, b * 2 + h + 1)
                ve.wait_ge(s_rest, b * 2 + h + 1)
                ve.sem_inc(s_md[i % 2], 1)

            def tail_use(b, i, what, k):
                o = sp_bank[i % 2]
                if what == "heads":
                    u = k % 2
                    o4 = o[:].rearrange("p (h w) -> p h w", w=VW)
                    ve.wait_ge(s_m, ready(b, i))
                    ve.reciprocal(rinv[:, u], o4[:, :, D]).then_inc(t_rinv, 1)
                    ve.wait_ge(t_rinv, b * 4 + k + 1)
                    ve.tensor_tensor(attn[:, u].rearrange("p (h d) -> p h d", d=D), o4[:, :, 0:D],
                                     rinv[:, u].rearrange("p (h o) -> p h o", o=1).to_broadcast([P, H, D]),
                                     ALU.mult).then_inc(t_attn, 1)
                    ve.wait_ge(t_attn, b * 4 + k + 1)
                    ve.sem_inc(s_md[i % 2], 1)
                if what == "out":
                    u = k % 2
                    r = rows[:, u]
                    ve.wait_ge(s_m, ready(b, i))
                    ve.wait_ge(t_x[u], b * 32 + (8 * (k - u) + 16))
                    ve.wait_ge(t_rowfree, b * 4 + k + 1)
                    ve.tensor_tensor(r[:, 0:E], o[:, 0:E], bob[:], ALU.add).then_inc(s_md[i % 2], 1)
                    ve.wait_ge(s_md[i % 2], free(b, i) + 1)
                    ve.scalar_tensor_tensor(out=r[:, 0:E], in0=r[:, 0:E], scalar=tg[:, 0:1], in1=xres[:, u],
                                            op0=ALU.mult, op1=ALU.add).then_inc(t_x1, 1)
                    ve.wait_ge(t_x1, b * 4 + k + 1)
                    ve.bn_stats(st2[:, u], r[:, 0:E]).then_inc(t_stat, 1)
                    wait_apart(ve, t_stat, b * 4 + k + 1)
                    ve.bn_aggr(mv2[:, u], st2[:, u]).then_inc(t_mv, 1)
                if what == "gate":
                    ve.wait_ge(s_m, ready(b, i))
                    t = (k[0] + 2) % 4
                    ve.tensor_copy(logit[:, t:t + len(k), :].rearrange("p t x -> p (t x)"),
                                   o[:, 0:len(k) * X]).then_inc(s_md[i % 2], 1)
                if what == "rank":
                    ve.wait_ge(s_m, ready(b, i))
                    place_tokens(b, i, o)

            def norm_row(b, k):
                u = k % 2
                r = rows[:, u]
                ve.wait_ge(t_rstd, b * 4 + k + 1)
                ve.tensor_scalar(r[:, E:2 * E], r[:, 0:E], mv2[:, u, 0:1], rstd2[:, u:u + 1],
                                 ALU.subtract, ALU.mult).then_inc(t_row, 1)

            def per_tile(ap):
                return ap.rearrange("p (t o) -> p t o", o=1).to_broadcast([P, QT, X])

            def per_expert(ap):
                return ap.rearrange("p (o x) -> p o x", o=1).to_broadcast([P, QT, X])

            ROUTE_LINKS = 9

            class Links:
                k = 0

            def link(ins, b):
                Links.k += 1
                ins.then_inc(r_dve, 1)
                ve.wait_ge(r_dve, b * ROUTE_LINKS + Links.k)

            def route_shift(b, i):
                ve.wait_ge(s_md[i % 2], free(b, i) + 1)
                Links.k = 0
                link(ve.tensor_reduce(mx[:], logit[:], AX.X, ALU.max), b)
                ve.tensor_tensor(logit[:], logit[:], per_tile(mx[:]), ALU.subtract).then_inc(r_sub, 1)

            def route_pick(b):
                ve.wait_ge(r_free, b + 1)
                ve.wait_ge(r_exp, b + 1)
                link(ve.tensor_reduce(sm[:], logit[:], AX.X, ALU.add), b)
                link(ve.tensor_reduce(em[:], logit[:], AX.X, ALU.max), b)
                link(ve.tensor_tensor(key[:], logit[:], per_tile(em[:]), ALU.is_equal), b)
                link(ve.tensor_tensor(key[:], key[:], per_expert(seven[:]), ALU.mult), b)
                link(ve.tensor_reduce(km[:], key[:], AX.X, ALU.max), b)
                ve.scalar_tensor_tensor(out=onehot[:], in0=key[:], scalar=live[:, ds(b, 1)], in1=per_tile(km[:]),
                                        op0=ALU.mult, op1=ALU.is_equal).then_inc(r_oh, 1)
                link(ve.reciprocal(wt[:], sm[:]), b)
                link(ve.tensor_tensor(wt[:], wt[:], em[:], ALU.mult), b)
                ve.tensor_scalar(pair[:].bitcast(F32)[:, :, 1], wt[:], tg[:, 1:2], None, ALU.mult).then_inc(r_wt, 1)

            def place_tokens(b, i, o):
                ve.tensor_tensor(place[:], o[:, 0:QT * X].rearrange("p (t x) -> p t x", x=X),
                                 per_expert(region[:]), ALU.add).then_inc(r_mx, 1)
                ve.wait_ge(r_mx, b + 1)
                ve.tensor_tensor(region[:], region[:], o[:, QT * X:(QT + 1) * X], ALU.add).then_inc(s_md[i % 2], 1)
                ve.tensor_tensor(place[:], place[:], onehot[:], ALU.mult).then_inc(r_st, 1)
                ve.wait_ge(r_st, b + 1)
                link(ve.tensor_reduce(posf[:], place[:], AX.X, ALU.add), b)
                assert Links.k == ROUTE_LINKS
                ve.tensor_scalar(posi[:], posf[:], dead[:, ds(b, 1)], None, ALU.add).then_inc(r_pair, 1)

            gate_i = next(i for i, (n, w, k) in enumerate(USES) if w == "gate")
            last_gate_i = next(i for i, (n, w, k) in enumerate(LAST_USES) if w == "gate")

            def step(b, n, uses, last=False):
                c = n - LE
                if 0 <= c and (c < TILES or not last) and c % 8 in DVE_COPIES:
                    g, qt, q2, h, j = tile_of(c)
                    ve.wait_ge(s_trans, b * TILES + c + 1)
                    if c >= 2 * TPG:
                        ve.wait_ge(s_pv, b * GROUPS + (c // TPG - 1))
                    ve.tensor_copy(pt[:, g % 2, :, j, q2 * P:(q2 + 1) * P],
                                   tr_bank[c % NTB][:].rearrange("p (c q) -> p c q", c=QT)).then_inc(s_cdve, 1)
                if n < TILES or not last:
                    g, qt, q2, h, j = tile_of(n)
                    m = n % TILES
                    if n % (TILES // 2) == 0:
                        ve.wait_ge(s_adjm, b * QT + (n // (TILES // 2) + 1) * (QT // 2))
                    if before(n, NB) is not None:
                        ve.wait_ge(s_trans, b * TILES + (before(n, NB) + 1))
                    wait_apart(ve, s_score, b * TILES + n + 1)
                    ve.tensor_tensor_reduce(out=prob[:, m % NB], in0=sc_bank[m % NS][:], in1=adjm[:, qt],
                                            scale=-1.0, scalar=BIG, op0=ALU.add, op1=ALU.min,
                                            accum_out=negmax[:, m % NB:m % NB + 1]).then_inc(s_masked, 1)
                if n >= LO + TPG and (n - LO) % TPG == 0:
                    g = (n - LO) // TPG - 1
                    ve.wait_ge(s_pv, b * GROUPS + g + 1)
                    ve.tensor_copy(o_sb[:, g % NG, g // NG], pv_bank[:, (g % 2) * HALF:(g % 2 + 1) * HALF]
                                   ).then_inc(s_osb, 1)
                for i, what, k in at_step(uses, n - VE_AT):
                    if what == "values":
                        values(b, i, k)
                    elif not what.startswith("next"):
                        tail_use(b, i, what, k)
                for i, what, k in at_step(uses, n - VE_QK_AT):
                    next_use(b, i, what, k, b + 1)
                if n in ROW_STEPS:
                    norm_row(b, ROW_STEPS[n])
                if n == SHIFT_STEP:
                    route_shift(b, last_gate_i if last else gate_i)
                if n == PICK_STEP:
                    route_pick(b)
                if not last:
                    if n == STATS_STEP:
                        norm_stats(b + 1)
                    if n == NORM_STEP:
                        norm(b + 1)

            norm_stats(0)
            norm(0)
            ve.wait_ge(s_md[0], 3)
            for j, (n, what, m) in enumerate(NEXT_USES):
                next_use(0, j - NEXT, what, m, 0)
                if what in ("next q", "next k"):
                    t = int(what == "next k")
                    ve.wait_ge(s_md[j % 2], free(0, j - NEXT) + 1)
                    ve.tensor_copy(parts[:, t, m, 1], rest[:]).then_inc(s_p1, 1)
                    ve.wait_ge(s_p1, 2 * m + t + 1)
                    ve.tensor_tensor(parts[:, t, m, 2], rest[:], parts[:, t, m, 1], ALU.subtract
                                     ).then_inc(s_parts, 1)
            ve.wait_ge(s_tg, 2)
            ve.wait_ge(s_bcast, 64)
            ve.wait_ge(s_vinit, 2)
            ve.wait_ge(s_const, 19)
            ve.wait_ge(t_ones, 2)
            ve.wait_ge(r_fill, 64)
            ve.sem_inc(t_rowfree, 2)
            ve.sem_inc(r_free, 1)
            ve.sem_inc(s_osb, 2)
            for n in range(LAG):
                step(0, n, USES)
            with ve.Fori(0, B - 1) as b:
                for n in range(LAG, LAG + TILES):
                    step(b, n, USES)
            for n in range(LAG, LO + TILES + 1):
                step(B - 1, n, LAST_USES, True)
            for i, (n, what, k) in enumerate(TAIL_A):
                if what == "normed":
                    norm_row(B, k)
                if what == "rank":
                    route_shift(B, i - 1 + LAST_SHIFT)
                    route_pick(B)
                tail_use(B, i + LAST_SHIFT, what, k)

            done = (B + 1) * ROUTE_LINKS

            def then(ins):
                nonlocal done
                done += 1
                ins.then_inc(r_dve, 1)
                ve.wait_ge(r_dve, done)

            last_rank = len(TAIL_A) - 1 + LAST_SHIFT
            ve.wait_ge(s_md[last_rank % 2], free(B, last_rank) + 1)
            then(ve.tensor_tensor(cnt[:], region[:], region0[:], ALU.subtract))
            then(ve.tensor_tensor(cmp_t[:], cnt[:].rearrange("p (x o) -> p x o", o=1).to_broadcast([P, X, NT]),
                                  thr[:].rearrange("p (o t) -> p o t", o=1).to_broadcast([P, X, NT]), ALU.is_gt))
            then(ve.tensor_reduce(tiles[:], cmp_t[:], AX.X, ALU.add))
            then(ve.tensor_scalar(span[:], tiles[:], -float(P), float(TOK), ALU.mult, ALU.add))
            src, dst = tiles, end
            step = 1
            while step < X:
                then(ve.tensor_copy(dst[:, 0:step], src[:, 0:step]))
                then(ve.tensor_tensor(dst[:, step:], src[:, step:], src[:, 0:X - step], ALU.add))
                src, dst = dst, end2 if dst is end else end
                step *= 2
            then(ve.tensor_tensor(cmp_s[:], slotn[:].rearrange("p (s o) -> p s o", o=1).to_broadcast([P, SLOTS_R, X]),
                                  src[:].rearrange("p (o x) -> p o x", o=1).to_broadcast([P, SLOTS_R, X]), ALU.is_ge))
            then(ve.tensor_reduce(ef[:], cmp_s[:], AX.X, ALU.add))
            then(ve.tensor_scalar(eid[:], ef[:], float(X - 1), None, ALU.min))
            then(ve.tensor_tensor(cmp_s[:], cmp_s[:],
                                  span[:].rearrange("p (o x) -> p o x", o=1).to_broadcast([P, SLOTS_R, X]), ALU.mult))
            then(ve.tensor_reduce(bf[:], cmp_s[:], AX.X, ALU.add))
            then(ve.scalar_tensor_tensor(out=bf[:], in0=slotn[:], scalar=float(P), in1=bf[:], op0=ALU.mult,
                                         op1=ALU.add))
            ve.tensor_scalar(base_i[:], bf[:], float(X * TOK), None, ALU.min).then_inc(r_eid, 1)

            def expert(s, i, u):
                e = ve.value_load(eid[0:1, ds(s, 1)], min_val=0, max_val=X - 1)
                ve.wait_ge(f_y, s + 1)
                ve.wait_ge(f_x1[u], i * 16 + 16)
                ve.tensor_tensor(ytmp[:, u], bank[4 * u + 3][:, 0:E],
                                 b2b[:, ds(e, 1), :].rearrange("p x e -> p (x e)"), ALU.add).then_inc(f_tmp, 1)
                ve.wait_ge(f_tmp, s + 3)
                ve.wait_ge(f_free, s + 1)
                ve.scalar_tensor_tensor(out=orow[:, u], in0=ytmp[:, u],
                                        scalar=slots[:].bitcast(F32)[:, ds(s, 1), 1], in1=rows[:, u, 0:E],
                                        op0=ALU.mult, op1=ALU.add).then_inc(f_out, 1)

            ve.sem_inc(f_free, 2)
            ve.sem_inc(f_tmp, 2)
            ve.wait_ge(r_eid, 1)
            ve.wait_ge(r_b2, 16)
            with ve.Fori(0, SLOTS // 2) as i:
                for u in range(2):
                    expert(i * 2 + u, i, u)
            expert(SLOTS - 1, SLOTS // 2, 0)


_INS = ["x", "ctx_1024", "mask_Bx1xSxS2_ik1", "g_xattn", "g_ffn", "L0_xattn_adj", "L0_xattn_Wq",
        "L0_xattn_bq", "L0_xattn_Wk", "L0_xattn_bk", "L0_xattn_Wv", "L0_xattn_bv", "L0_xattn_Wo",
        "L0_xattn_bo", "L0_ffn_gate_w", "L0_ffn_w1", "L0_ffn_b1", "L0_ffn_w2", "L0_ffn_b2"]


def kernel(**inputs):
    import numpy as np
    import concourse.bacc as bacc
    from concourse.bass_utils import run_bass_kernel_spmd

    nc = bacc.Bacc("TRN2", target_bir_lowering=False, num_devices=1)
    arrays, args = {}, []
    for name in _INS:
        a = np.ascontiguousarray(inputs[name])
        arrays[f"in_{name}"] = a
        args.append(nc.dram_tensor(f"in_{name}", a.shape, mybir.dt.from_np(a.dtype), kind="ExternalInput").ap())
    shape = inputs["x"].shape
    out = nc.dram_tensor("out_y", shape, F32, kind="ExternalOutput").ap()
    build(nc, *args, out)
    r = run_bass_kernel_spmd(nc, [arrays], core_ids=[0])
    return r.results[0]["out_y"]
```
